# Optimizing a Trainium2 kernel written in Bass

```python
import numpy as np
import jax
import jax.numpy as jnp

def _softmax(x, axis=-1):
    return jax.nn.softmax(x, axis=axis)

def _gelu(x):
    return jax.nn.gelu(x, approximate=True)

def _silu(x):
    return jax.nn.silu(x)

def _sigmoid(x):
    return jax.nn.sigmoid(x)

def _layernorm(x, axis=-1, eps=1e-05):
    m = jnp.mean(x, axis=axis, keepdims=True)
    v = jnp.var(x, axis=axis, keepdims=True)
    return (x - m) / jnp.sqrt(v + eps)

def _scatter_add(tgt, idx, src, axis=0):
    return tgt.at[idx].add(src)

def _segment_sum(src, seg, n):
    return jax.ops.segment_sum(src, seg, n)
kernel_name = 'mk_vit_tower_d1_tok_img256_r4_ca8fe8'

def setup_inputs(seed: int=0):
    np.random.seed(seed)
    _w = jnp.asarray

    def _rec_inputs():
        import jax
        import jax.numpy as jnp
        _rk = jax.random.key(seed)
        x = 7.22013e-05 + 1.00017 * jax.random.normal(jax.random.fold_in(_rk, 1), (16, 1, 224, 224), jnp.float32)
        return x
    x = _rec_inputs()

    def _L0_tok_setup():
        import jax, jax.numpy as jnp
        import numpy as np
        P = 8
        C = 1
        D = 64
        key = jax.random.key(seed)
        k1, k2, k3 = jax.random.split(key, 3)
        x = jax.random.normal(k1, (128, C, 64, 64), dtype=jnp.float32)
        patch_dim = P * P * C
        bound = 1.0 / np.sqrt(patch_dim)
        W = jax.random.uniform(k2, (D, patch_dim), dtype=jnp.float32, minval=-bound, maxval=bound)
        b = jax.random.uniform(k3, (D,), dtype=jnp.float32, minval=-bound, maxval=bound)
        return {'x': x, 'W': W, 'b': b}
    _L0_tok_all = _L0_tok_setup()
    _L0_tok_in = {k: v for k, v in _L0_tok_all.items() if k in ('W', 'b')}
    del _L0_tok_all

    def _L0_attn_setup():
        import jax, jax.numpy as jnp
        import numpy as np
        D = 64
        L = 2
        B, S = (8, 1024)
        LR = 0.001
        WD = 0.01
        MAX_ALR = 0.1
        EPS = 1e-08

        def _lmm(Ws, bs, x):
            for i in range(L):
                x = x + jax.nn.silu(x @ Ws[i] + bs[i])
            return x

        def _reference_tuple_inner(x, Wk, Wq, Wv, Wlr, blr, Ws, bs):
            keys = x @ Wk
            queries = x @ Wq
            values = x @ Wv
            alr = (jax.nn.sigmoid(x @ Wlr + blr) * MAX_ALR).reshape(-1)

            def loss_fn(params):
                Ws_, bs_ = params
                preds = _lmm(Ws_, bs_, keys).reshape(-1, D)
                tgt = values.reshape(-1, D)
                per_tok = jnp.mean((preds - tgt) ** 2, axis=-1)
                return jnp.sum(per_tok * alr)
            gWs, gbs = jax.grad(loss_fn)((Ws, bs))

            def adamw_step(p, g):
                return p * (1.0 - LR * WD) - LR * g / (jnp.sqrt(g * g) + EPS)
            nWs = adamw_step(Ws, gWs)
            nbs = adamw_step(bs, gbs)
            retrieved = _lmm(nWs, nbs, queries)
            return (retrieved, -gWs, -gbs)
        key = jax.random.key(seed)
        ks = jax.random.split(key, 9)
        scale = 0.05
        return {'x': jax.random.normal(ks[0], (B, S, D), dtype=jnp.float32), 'Wk': jax.random.normal(ks[1], (D, D), dtype=jnp.float32) * scale, 'Wq': jax.random.normal(ks[2], (D, D), dtype=jnp.float32) * scale, 'Wv': jax.random.normal(ks[3], (D, D), dtype=jnp.float32) * scale, 'Wlr': jax.random.normal(ks[4], (D, 1), dtype=jnp.float32) * scale, 'blr': jnp.zeros((1,), dtype=jnp.float32), 'Ws': jax.random.normal(ks[5], (L, D, D), dtype=jnp.float32) * scale, 'bs': jnp.zeros((L, D), dtype=jnp.float32)}
    _L0_attn_all = _L0_attn_setup()
    _L0_attn_in = {k: v for k, v in _L0_attn_all.items() if k in ('Wk', 'Wq', 'Wv', 'Wlr', 'blr', 'Ws', 'bs')}
    del _L0_attn_all

    def _L0_ffn_setup():
        import jax, jax.numpy as jnp
        import numpy as np
        B, T, C = (64, 96, 64)
        NH, NKV = (4, 2)
        HD = C // NH
        NREP = NH // NKV
        NE, TOPK = (8, 2)
        HID = int(8 / 3 * C)
        EPS_RMS = 1e-06

        def _rope_tables(t_len):
            inv_freq = 1.0 / 10000.0 ** (np.arange(0, HD, 2, dtype=np.float32) / HD)
            t = np.arange(t_len, dtype=np.float32)
            freqs = np.outer(t, inv_freq)
            emb = np.concatenate([freqs, freqs], axis=-1)
            return (jnp.asarray(np.cos(emb)), jnp.asarray(np.sin(emb)))

        def _rotate_half(x):
            h = x.shape[-1] // 2
            return jnp.concatenate([-x[..., h:], x[..., :h]], axis=-1)

        def _rmsnorm(v, w):
            return v * jax.lax.rsqrt(jnp.mean(v * v, axis=-1, keepdims=True) + EPS_RMS) * w
        key = jax.random.key(seed)
        ks = jax.random.split(key, 10)
        s = lambda k, shape: jax.random.normal(k, shape, jnp.float32) * 0.02
        return {'x': jax.random.normal(ks[0], (B, T, C), jnp.float32), 'ln1_w': jnp.ones((C,), jnp.float32), 'ln2_w': jnp.ones((C,), jnp.float32), 'wq': s(ks[1], (NH * HD, C)), 'wk': s(ks[2], (NKV * HD, C)), 'wv': s(ks[3], (NKV * HD, C)), 'wo': s(ks[4], (C, C)), 'router_w': s(ks[5], (NE, C)), 'w1': s(ks[6], (NE, HID, C)), 'w2': s(ks[7], (NE, C, HID)), 'w3': s(ks[8], (NE, HID, C))}
    _L0_ffn_all = _L0_ffn_setup()
    _L0_ffn_in = {k: v for k, v in _L0_ffn_all.items() if k in ('ln1_w', 'ln2_w', 'wq', 'wk', 'wv', 'wo', 'router_w', 'w1', 'w2', 'w3')}
    del _L0_ffn_all
    return {'x': x, 'L0_tok_W': _L0_tok_in['W'], 'L0_tok_b': _L0_tok_in['b'], 'L0_attn_Wk': _L0_attn_in['Wk'], 'L0_attn_Wq': _L0_attn_in['Wq'], 'L0_attn_Wv': _L0_attn_in['Wv'], 'L0_attn_Wlr': _L0_attn_in['Wlr'], 'L0_attn_blr': _L0_attn_in['blr'], 'L0_attn_Ws': _L0_attn_in['Ws'], 'L0_attn_bs': _L0_attn_in['bs'], 'L0_ffn_ln1_w': _L0_ffn_in['ln1_w'], 'L0_ffn_ln2_w': _L0_ffn_in['ln2_w'], 'L0_ffn_wq': _L0_ffn_in['wq'], 'L0_ffn_wk': _L0_ffn_in['wk'], 'L0_ffn_wv': _L0_ffn_in['wv'], 'L0_ffn_wo': _L0_ffn_in['wo'], 'L0_ffn_router_w': _L0_ffn_in['router_w'], 'L0_ffn_w1': _L0_ffn_in['w1'], 'L0_ffn_w2': _L0_ffn_in['w2'], 'L0_ffn_w3': _L0_ffn_in['w3']}

def reference(x, L0_tok_W, L0_tok_b, L0_attn_Wk, L0_attn_Wq, L0_attn_Wv, L0_attn_Wlr, L0_attn_blr, L0_attn_Ws, L0_attn_bs, L0_ffn_ln1_w, L0_ffn_ln2_w, L0_ffn_wq, L0_ffn_wk, L0_ffn_wv, L0_ffn_wo, L0_ffn_router_w, L0_ffn_w1, L0_ffn_w2, L0_ffn_w3):
    import jax
    import jax.numpy as jnp

    def _L0_tok_ref(x, W, b):
        import jax, jax.numpy as jnp
        import numpy as np
        P = 8
        C = 1
        D = 64
        B, c, h, w = x.shape
        p = P
        xp = x.reshape(B, c, h // p, p, w // p, p)
        xp = jnp.transpose(xp, (0, 2, 4, 3, 5, 1))
        xp = xp.reshape(B, h // p * (w // p), p * p * c)
        return jnp.einsum('bnk,dk->bnd', xp, W) + b

    def _L0_attn_ref(x, Wk, Wq, Wv, Wlr, blr, Ws, bs):
        import jax, jax.numpy as jnp
        import numpy as np
        D = 64
        L = 2
        B, S = (8, 1024)
        LR = 0.001
        WD = 0.01
        MAX_ALR = 0.1
        EPS = 1e-08

        def _lmm(Ws, bs, x):
            for i in range(L):
                x = x + jax.nn.silu(x @ Ws[i] + bs[i])
            return x

        def _reference_tuple_inner(x, Wk, Wq, Wv, Wlr, blr, Ws, bs):
            keys = x @ Wk
            queries = x @ Wq
            values = x @ Wv
            alr = (jax.nn.sigmoid(x @ Wlr + blr) * MAX_ALR).reshape(-1)

            def loss_fn(params):
                Ws_, bs_ = params
                preds = _lmm(Ws_, bs_, keys).reshape(-1, D)
                tgt = values.reshape(-1, D)
                per_tok = jnp.mean((preds - tgt) ** 2, axis=-1)
                return jnp.sum(per_tok * alr)
            gWs, gbs = jax.grad(loss_fn)((Ws, bs))

            def adamw_step(p, g):
                return p * (1.0 - LR * WD) - LR * g / (jnp.sqrt(g * g) + EPS)
            nWs = adamw_step(Ws, gWs)
            nbs = adamw_step(bs, gbs)
            retrieved = _lmm(nWs, nbs, queries)
            return (retrieved, -gWs, -gbs)
        return _reference_tuple_inner(x, Wk, Wq, Wv, Wlr, blr, Ws, bs)[0]

    def _L0_ffn_ref(x, ln1_w, ln2_w, wq, wk, wv, wo, router_w, w1, w2, w3):
        import jax, jax.numpy as jnp
        import numpy as np
        B, T, C = (64, 96, 64)
        NH, NKV = (4, 2)
        HD = C // NH
        NREP = NH // NKV
        NE, TOPK = (8, 2)
        HID = int(8 / 3 * C)
        EPS_RMS = 1e-06

        def _rope_tables(t_len):
            inv_freq = 1.0 / 10000.0 ** (np.arange(0, HD, 2, dtype=np.float32) / HD)
            t = np.arange(t_len, dtype=np.float32)
            freqs = np.outer(t, inv_freq)
            emb = np.concatenate([freqs, freqs], axis=-1)
            return (jnp.asarray(np.cos(emb)), jnp.asarray(np.sin(emb)))

        def _rotate_half(x):
            h = x.shape[-1] // 2
            return jnp.concatenate([-x[..., h:], x[..., :h]], axis=-1)

        def _rmsnorm(v, w):
            return v * jax.lax.rsqrt(jnp.mean(v * v, axis=-1, keepdims=True) + EPS_RMS) * w
        Bx, Tx, Cx = x.shape
        h = _rmsnorm(x, ln1_w)
        q = (h @ wq.T).reshape(Bx, Tx, NH, HD).transpose(0, 2, 1, 3)
        k = (h @ wk.T).reshape(Bx, Tx, NKV, HD).transpose(0, 2, 1, 3)
        v = (h @ wv.T).reshape(Bx, Tx, NKV, HD).transpose(0, 2, 1, 3)
        cos, sin = _rope_tables(Tx)
        cos, sin = (cos[None, None], sin[None, None])
        q = q * cos + _rotate_half(q) * sin
        k = k * cos + _rotate_half(k) * sin
        k = jnp.repeat(k, NREP, axis=1)
        v = jnp.repeat(v, NREP, axis=1)
        scores = jnp.einsum('bhtd,bhsd->bhts', q, k) / jnp.sqrt(jnp.float32(HD))
        causal = jnp.tril(jnp.ones((Tx, Tx), dtype=bool))
        scores = jnp.where(causal[None, None], scores, jnp.float32(-1e+30))
        att = jax.nn.softmax(scores, axis=-1)
        y = jnp.einsum('bhts,bhsd->bhtd', att, v).transpose(0, 2, 1, 3).reshape(Bx, Tx, Cx)
        x = x + y @ wo.T
        flat = _rmsnorm(x, ln2_w).reshape(-1, Cx)
        probs = jax.nn.softmax(flat @ router_w.T, axis=-1)
        tp, ti = jax.lax.top_k(probs, TOPK)
        tp = tp / (jnp.sum(tp, axis=-1, keepdims=True) + 1e-09)
        weights = jnp.sum(tp[..., None] * jax.nn.one_hot(ti, NE, dtype=flat.dtype), axis=1)
        out = jnp.zeros_like(flat)
        for e in range(NE):
            hh = jax.nn.silu(flat @ w1[e].T) * (flat @ w3[e].T)
            out = out + weights[:, e:e + 1] * (hh @ w2[e].T)
        return x + out.reshape(Bx, Tx, Cx)
    h = _L0_tok_ref(x, L0_tok_W, L0_tok_b)
    h = h + _L0_attn_ref(_layernorm(h, axis=-1), L0_attn_Wk, L0_attn_Wq, L0_attn_Wv, L0_attn_Wlr, L0_attn_blr, L0_attn_Ws, L0_attn_bs)
    h = h + _L0_ffn_ref(_layernorm(h, axis=-1), L0_ffn_ln1_w, L0_ffn_ln2_w, L0_ffn_wq, L0_ffn_wk, L0_ffn_wv, L0_ffn_wo, L0_ffn_router_w, L0_ffn_w1, L0_ffn_w2, L0_ffn_w3)
    return h

_drawn_inputs = setup_inputs


def setup_inputs(seed=0):
    import zlib

    import numpy as np

    out = dict(_drawn_inputs(seed))
    spreads = {'L0_attn_bs': (0.0, 0.1), 'L0_ffn_ln1_w': (1.0, 0.6), 'L0_ffn_ln2_w': (1.0, 0.6)}
    factors = {'L0_attn_Wk': 8.0,
     'L0_attn_Wv': 8.0,
     'L0_attn_Wlr': 8.0,
     'L0_ffn_wq': 8.0,
     'L0_ffn_wk': 8.0,
     'L0_ffn_wv': 8.0,
     'L0_ffn_wo': 8.0,
     'L0_ffn_router_w': 8.0,
     'L0_ffn_w1': 8.0,
     'L0_ffn_w2': 8.0,
     'L0_ffn_w3': 8.0}
    for name, (base, spread) in spreads.items():
        noise = np.random.default_rng([zlib.crc32(name.encode()), seed]).standard_normal(out[name].shape)
        drawn = base * np.exp(spread * noise) if base else spread * noise
        out[name] = jnp.asarray(drawn.astype(out[name].dtype))
    for name, factor in factors.items():
        out[name] = (out[name] * factor).astype(out[name].dtype)
    return out
```

```python
from contextlib import ExitStack

import numpy as np

import concourse.bass as bass
from concourse import mybir

F32 = mybir.dt.float32
F32R = mybir.dt.float32r
BF16 = mybir.dt.bfloat16
ALU = mybir.AluOpType
ACT = mybir.ActivationFunctionType
AX = mybir.AxisListType

IMAGES = 16
SIDE = 28
TOK = SIDE * SIDE
TP = 112
NT = TOK // TP
D = 64
PATCH = 8
NH, NKV, HD = 4, 2, 16
QK = (NH + NKV) * HD
NE, HID = 8, 170
PAIRS = NE // 2
MAIN = 128
TAIL = HID - MAIN
TAIL_W = 64 + TAIL
PAIR_W = 2 * MAIN + TAIL_W
CHUNKS = [(0, 4), (4, 7)]
BANK = 512
LR, WD, MAX_ALR, EPS_ADAM = 0.001, 0.01, 0.1, 1e-8
EPS_LN, EPS_RMS, EPS_TOP = 1e-5, 1e-6, 1e-9
NEG = -1e30
Q_ROWS = 96

C_ID = 0
C_MASK = C_ID + 128
C_SELH = C_MASK + TP
C_SELL = C_SELH + 3 * 128
C_PAIR = C_SELL + 3 * 128
C_DEN = C_PAIR + PAIRS * 128
C_FOLD = C_DEN + 128
C_LOW64 = C_FOLD + 64
C_LOW32 = C_LOW64 + 1
C_MAXROW = C_LOW32 + 1
C_RANK = C_MAXROW + NH
C_HALF = C_RANK + NT * NE
C_ALL = C_HALF + NT


def shape_constants():
    c = np.zeros((128, C_ALL), np.float32)
    c[:, C_ID:C_ID + 128] = np.eye(128)
    c[:TP, C_MASK:C_MASK + TP] = np.triu(np.full((TP, TP), NEG), 1)
    for out in range(3):
        for r in range(128):
            part, d = (r % 64) // 16, r % 16
            src = (out * 2 + r // 64) * HD + d
            low = part % 2 if out < 2 else part // 2
            c[src, (C_SELL if low else C_SELH) + out * 128 + r] = 1
    for p in range(PAIRS):
        for r in range(128):
            e = 2 * p + r // 64
            c[e, C_PAIR + p * 128 + r] = 1
            c[32 + e, C_PAIR + p * 128 + r] = 1
    for r in range(128):
        c[32 * (r // 32) + HD, C_DEN + r] = 1
    c[:, C_FOLD:C_FOLD + 64] = np.concatenate([np.eye(64), np.eye(64)])
    c[64:, C_LOW64] = -1
    c[32:64, C_LOW32] = -1
    for h in range(NH):
        c[64 + h, C_MAXROW + h] = -1
    c[:, C_RANK:C_RANK + NT * NE] = np.tile(np.arange(NE, 0, -1), NT)
    c[:, C_HALF:C_HALF + NT] = -0.5
    inv = 1.0 / 10000.0 ** (np.arange(0, HD, 2, dtype=np.float32) / HD)
    freqs = np.outer(np.arange(TOK, dtype=np.float32), inv)
    emb = np.concatenate([freqs, freqs], -1)
    sign = np.where(np.arange(HD) < HD // 2, -1, 1).astype(np.float32)
    cos = np.tile(np.cos(emb).T, (NH + NKV, 1))
    sin = np.tile((np.sin(emb) * sign).T, (NH + NKV, 1))
    return c, np.stack([cos, sin], 1).astype(np.float32)


class Steps:

    def __init__(self, eng, sem):
        self.eng, self.sem, self.start, self.n, self.base = eng, sem, 0, 0, 0

    def loop(self, i, per):
        self.start += self.n
        self.per, self.n, self.base = per, 0, self.start + i * per

    def unloop(self, rounds):
        assert self.n == self.per, (self.n, self.per)
        self.start += rounds * self.per
        self.n, self.base = 0, self.start

    def link(self, ins):
        self.n += 1
        ins.then_inc(self.sem, 1)
        self.eng.wait_ge(self.sem, self.base + self.n)


def vit_block(nc, A):
    ctx = ExitStack()
    with ctx:
        def sb(name, shape, dt=F32):
            return ctx.enter_context(nc.sbuf_tensor(name, shape, dt))

        def sem(name):
            return ctx.enter_context(nc.semaphore(name))

        con = sb("con", [128, C_ALL])
        rope = sb("rope", [QK, 2, TOK])
        sel = sb("sel", [128, 6, 128], F32R)
        selp = sb("selp", [40, PAIRS, 128], F32R)
        idb = sb("idb", [TP, TP], BF16)
        maskb = sb("maskb", [TP, TP], BF16)
        ident = con[:, C_ID:C_ID + 128]
        tokw = sb("tokw", [D + 1, D])
        wk_t = sb("wk_t", [D, D])
        wq_t = sb("wq_t", [D, D])
        w1l_t = sb("w1l_t", [D, D])
        ws = sb("ws", [D + 1, 2, D])
        nws = sb("nws", [D + 1, 2, D])
        wproj = sb("wproj", [D + 1, 194])
        wqproj = sb("wqproj", [D + 1, 2 * D])
        NA = 2 * QK + NKV * HD
        NB = NE
        araw = sb("araw", [128, NA])
        wah = sb("wah", [128, NA], F32R)
        wal = sb("wal", [128, NA], F32R)
        rraw = sb("rraw", [128, NB])
        wrh = sb("wrh", [128, NB], F32R)
        wrl = sb("wrl", [128, NB], F32R)
        lnw = sb("lnw", [128, 2])
        wmh = sb("wmh", [128, 2 * PAIRS * PAIR_W], F32R)
        wml = sb("wml", [128, 2 * PAIRS * PAIR_W], F32R)
        w2 = sb("w2", [128, 3 * PAIRS, D])
        wo = sb("wo", [128, D])

        h_all = sb("h_all", [TP, IMAGES * NT * D])
        x1_store = nc.dram_tensor("x1_store", (TP, IMAGES, NT * D), F32, kind="Internal").ap()
        gacc = sb("gacc", [D + 1, 2, D])
        gtmp = sb("gtmp", [D + 1, 2, D])

        pv = sb("pv", [128, TOK])
        patch = pv[0:D + 1, :]
        x1 = sb("x1", [TP, NT, D])
        xt = sb("xt", [D + 1, TOK])
        at = sb("at", [D + 1, TOK])
        a1 = sb("a1", [TP, NT, D + 2])
        ke = sb("ke", [TP, NT, D + 2])
        tm = [sb(f"tm{n}", [TP, NT, D]) for n in range(6)]
        xc, sq, sg, si, sp1, sp2 = tm
        dp = sb("dp", [TP, NT, D])
        dz = sb("dz", [TP, NT, D])
        dz1 = sb("dz1", [TP, NT, D])
        st = sb("st", [TP, 8, NT])
        h2, x2, res = dp, dz1, dz
        xd = sb("xd", [TP, NT, 2, D])
        xh = sb("xh", [128, TOK], F32R)
        xs = sb("xs", [128, TOK], F32R)
        qk = sb("qk", [QK, TOK])
        qkh = sb("qkh", [QK, TOK], F32R)
        qkl = sb("qkl", [QK, TOK], F32R)
        qx = sb("qx", [Q_ROWS, NH, TOK], F32R)
        kx = sb("kx", [Q_ROWS, NKV, TOK], F32R)
        v1 = sb("v1", [TP, NT, NKV, 32])
        mx = sb("mx", [TP, NT, 32])
        pt = sb("pt", [128, 2, NH, TOK])
        mraw = pt[:].rearrange("p a h n -> p (a h n)")[:, 0:2 * PAIRS * PAIR_W]
        rden = sb("rden", [128, TOK])
        yn = sb("yn", [128, TOK])
        qk_sin = yn[0:QK, :]
        rt = sb("rt", [TP, 8, NT, NE])
        wt = sb("wt", [TP, NT, 40])
        wth = xh[0:40, :]
        wts = sb("wts", [40, TOK], F32R)
        bw = sb("bw", [128, 2, 448])
        su = sb("su", [128, 2, 448])
        hh = sb("hh", [128, 3, 448])
        zz = sb("zz", [128, 2, 448])
        zacc = rden

        P = ctx.enter_context(nc.psum_tensor("P", [128, 8, BANK], F32))
        flat = P[:, :, :].rearrange("p b n -> p (b n)")

        def tiles(b):
            return P[0:TP, b, 0:NT * D].rearrange("p (t f) -> p t f", f=D)

        def tok_cols(c):
            t0, t1 = CHUNKS[c]
            return slice(t0 * TP, t1 * TP)

        def width(c):
            return (CHUNKS[c][1] - CHUNKS[c][0]) * TP

        names = """loaded patch_in patch_used set_done weights_split wz0_ps wproj_ready h_ps h_saved var_ready
            rstd_ready x1_ready x1_stored xt_ps xt_ready proj_ps sig1 keys_saved alr_ready si1_ready
            slope1_ready a1_ready a1_used z2_ps sig2 si2_ready slope2_ready dz2_ready da_ps dz1_ready
            grad_ps dve_steps grads_summed nws_ready wz_ps wqproj_ready x1_back x1_free pre_ps silu_z
            ar_ready silu_z2 q_var q_rstd xd_ready xd_ps xh_ready xs_ready qk_ps v_saved rope_done
            qkh_ready qkl_ready spread_ps qx_saved qx_zero smax_ps smax_read mx_ready mxt_ps mrow_act
            mrow_dve st_ps exp_done diag_done pv_ps pv_saved den_ps rden_ready yn_ready wo_ps logit_ps
            logit_read exp_r wt_ready wt_ps wth_ready wts_ready bw_ps bw_saved h1_ps silu_done h3_ps
            hh_ready y_ps z_ready z_added fold_ps out_ready out_sent pool_steps pool_set waited""".split()
        S = {n: sem(n) for n in names}

        block = ctx.enter_context(nc.Block())

        D1, D2 = 9, 39

        @block.sync
        def _(sp):
            for dst, src in ((con[:], A["con"]), (rope[:], A["rope"]), (tokw[:], A["tokw"]),
                             (wk_t[:], A["wk_t"]), (wq_t[:], A["wq_t"]), (w1l_t[:], A["w1l_t"]), (ws[:], A["ws"]),
                             (wproj[:, 64:193], A["wproj"]), (wqproj[:, D:], A["wqp"]),
                             (araw[0:64, :], A["attnw"]), (araw[64:128, :], A["attnw"]),
                             (rraw[0:64, :], A["router"]), (rraw[64:128, :], A["router"]),
                             (lnw[0:64, :], A["lnw"]), (lnw[64:128, :], A["lnw"]),
                             (mraw[0:64], A["w13"]), (mraw[64:128], A["w13"]),
                             (w2[:], A["w2"]), (wo[:], A["wo"])):
                sp.dma_start(dst, src).then_inc(S["loaded"], 16)
            with sp.Fori(0, IMAGES) as i:
                sp.wait_ge(S["patch_used"], i + 1)
                sp.dma_start(patch[0:D, :], A["patches"][:, bass.ds(i * TOK, TOK)]).then_inc(S["patch_in"], 16)
                sp.wait_ge(S["x1_ready"], i + 1)
                sp.dma_start(x1_store[:, bass.ds(i, 1), :].rearrange("p a n -> p (a n)"),
                             x1[:].rearrange("p t f -> p (t f)")).then_inc(S["x1_stored"], 16)
            sp.wait_ge(S["x1_stored"], 16 * IMAGES + 16)
            sp.wait_ge(S["weights_split"], 1)
            with sp.Fori(0, IMAGES) as i:
                sp.wait_ge(S["x1_free"], i + 1)
                sp.dma_start(x1[:].rearrange("p t f -> p (t f)"),
                             x1_store[:, bass.ds(i, 1), :].rearrange("p a n -> p (a n)")).then_inc(S["x1_back"], 16)
                sp.wait_ge(S["out_ready"], i + 1)
                sp.dma_start(A["out"][:, bass.ds(i * NT, NT), :], res[:]).then_inc(S["out_sent"], 16)
            sp.wait_ge(S["out_sent"], 16 * IMAGES + 16)

        N_LOADS = 19

        @block.gpsimd
        def _(pool):
            setting = Steps(pool, S["pool_set"])
            for ap, value in ((patch[D:D + 1, :], 1.0), (xt[D:D + 1, :], 1.0), (at[D:D + 1, :], 1.0),
                              (a1[:, :, D:], 1.0), (ke[:, :, D:], 1.0), (v1[:], 0.0), (mx[:], 0.0), (wt[:], 0.0),
                              (gacc[:], 0.0), (kx[64:96, :, :].bitcast(F32), 1.0), (wproj[:, 193:194], 0.0),
                              (v1[:, :, :, HD:HD + 1], 1.0)):
                setting.link(nc.gpsimd.memset(ap, value))
            pool.drain().then_inc(S["set_done"], 1)
            pool.wait_ge(S["loaded"], 16 * N_LOADS)
            half = con[0:TP, C_HALF:C_HALF + NT]
            with pool.Fori(0, IMAGES) as i:
                pool.wait_ge(S["var_ready"], i + 1)
                nc.gpsimd.tensor_tensor(st[:, 3, :], st[:, 2, :], half, ALU.pow).then_inc(S["rstd_ready"], 1)
                pool.wait_ge(S["si1_ready"], i + 1)
                nc.gpsimd.tensor_tensor(sp1[:], si[:], sg[:], ALU.mult).then_inc(S["pool_steps"], 1)
                nc.gpsimd.tensor_tensor(sq[:], si[:], sg[:], ALU.add).then_inc(S["pool_steps"], 1)
                pool.wait_ge(S["pool_steps"], 2 + 4 * i)
                nc.gpsimd.tensor_tensor(sp1[:], sq[:], sp1[:], ALU.subtract).then_inc(S["slope1_ready"], 1)
                pool.wait_ge(S["si2_ready"], i + 1)
                nc.gpsimd.tensor_tensor(sp2[:], si[:], sg[:], ALU.mult).then_inc(S["pool_steps"], 1)
                nc.gpsimd.tensor_tensor(sq[:], si[:], sg[:], ALU.add).then_inc(S["pool_steps"], 1)
                pool.wait_ge(S["pool_steps"], 4 + 4 * i)
                nc.gpsimd.tensor_tensor(sp2[:], sq[:], sp2[:], ALU.subtract).then_inc(S["slope2_ready"], 1)
            with pool.Fori(0, IMAGES) as i:
                for k in range(3):
                    pool.wait_ge(S["q_var"], 3 * i + k + 1)
                    nc.gpsimd.tensor_tensor(st[:, 3, :], st[:, 2, :], half, ALU.pow).then_inc(S["q_rstd"], 1)
                    if k == 1:
                        pool.wait_ge(S["q_rstd"], 3 * i + 2)
                        pool.sem_inc(S["waited"], 1)
                        nc.gpsimd.memset(qx[64:96, :, :].bitcast(F32), 0.0).then_inc(S["qx_zero"], 1)
                        for kb in range(NT):
                            for hp in range(2):
                                pool.wait_ge(S["exp_done"], i * 22 + first_piece(kb) * 2 + hp + 1)
                                pool.sem_inc(S["waited"], 1)
                                d = pt[0:TP, kb % 2, 2 * hp:2 * hp + 2, kb * TP:(kb + 1) * TP]
                                nc.gpsimd.affine_select(out=d, in_=d, compare_op=ALU.is_ge, fill=0.0, base=0,
                                                        pattern=[[0, 2], [1, TP]], channel_multiplier=-1
                                                        ).then_inc(S["diag_done"], 1)
                        pool.wait_ge(S["rden_ready"], i + 1)
                        pool.wait_ge(S["pv_saved"], 2 * i + 2)
                        nc.gpsimd.tensor_tensor(yn[:], pv[:], rden[:], ALU.mult).then_inc(S["yn_ready"], 1)
                for c in range(2):
                    for p in range(PAIRS):
                        n = c * PAIRS + p
                        pool.wait_ge(S["z_ready"], 8 * i + n + 1)
                        if p == 0:
                            pool.sem_inc(S["waited"], 1)
                        w, cols = width(c), tok_cols(c)
                        if p == 0:
                            ins = nc.gpsimd.tensor_copy(zacc[:, cols], zz[:, n % 2, 0:w])
                        else:
                            pool.wait_ge(S["z_added"], 8 * i + n)
                            ins = nc.gpsimd.tensor_tensor(zacc[:, cols], zacc[:, cols], zz[:, n % 2, 0:w], ALU.add)
                        ins.then_inc(S["z_added"], 1)

        @block.tensor
        def _(pe):
            mm = nc.tensor.matmul

            def transposes(src, rows, b, ready):
                pe.sem_inc(S["waited"], 1)
                for c, (t0, t1) in enumerate(CHUNKS):
                    for t in range(t0, t1):
                        last = nc.tensor.transpose(P[0:rows, b + c, (t - t0) * TP:(t - t0 + 1) * TP],
                                                   src(t), ident[0:TP, 0:TP])
                    last.then_inc(ready, 1)

            pe.wait_ge(S["loaded"], 16 * N_LOADS)
            pe.wait_ge(S["set_done"], 1)
            mm(P[0:D, 0, 0:D], wk_t[:], ws[0:D, 0, :], start=True, stop=True).then_inc(S["wz0_ps"], 1)
            pe.wait_ge(S["wproj_ready"], 1)
            with pe.Fori(0, IMAGES) as i:
                pe.wait_ge(S["patch_in"], 16 * i + 16)
                for t in range(NT):
                    last = mm(P[0:TP, 0, t * D:(t + 1) * D], patch[:, t * TP:(t + 1) * TP], tokw[:],
                              start=True, stop=True)
                last.then_inc(S["h_ps"], 1)
                pe.wait_ge(S["x1_ready"], i + 1)
                transposes(lambda t: x1[:, t, :], D, 1, S["xt_ps"])
                pe.wait_ge(S["xt_ready"], 6 * i + 2)
                for t in range(NT):
                    last = mm(flat[0:TP, 3 * BANK + t * 256:3 * BANK + t * 256 + 194], xt[:, t * TP:(t + 1) * TP],
                              wproj[:], start=True, stop=True)
                last.then_inc(S["proj_ps"], 1)
                pe.wait_ge(S["a1_ready"], i + 1)
                transposes(lambda t: a1[:, t, 0:D], D, 1, S["xt_ps"])
                pe.wait_ge(S["xt_ready"], 6 * i + 4)
                for t in range(NT):
                    last = mm(P[0:TP, 0, t * D:(t + 1) * D], at[:, t * TP:(t + 1) * TP], ws[:, 1, :],
                              start=True, stop=True)
                last.then_inc(S["z2_ps"], 1)
                pe.wait_ge(S["dz2_ready"], i + 1)
                transposes(lambda t: dz[:, t, :], D, 1, S["xt_ps"])
                for t in range(NT):
                    mm(P[0:D + 1, 7, D:2 * D], a1[:, t, 0:D + 1], dz[:, t, :], start=(t == 0), stop=(t == NT - 1))
                pe.wait_ge(S["xt_ready"], 6 * i + 6)
                for t in range(NT):
                    last = mm(P[0:TP, 0, t * D:(t + 1) * D], xt[0:D, t * TP:(t + 1) * TP], w1l_t[:],
                              start=True, stop=True)
                last.then_inc(S["da_ps"], 1)
                pe.wait_ge(S["dz1_ready"], i + 1)
                pe.wait_ge(S["keys_saved"], i + 1)
                for t in range(NT):
                    last = mm(P[0:D + 1, 7, 0:D], ke[:, t, 0:D + 1], dz1[:, t, :], start=(t == 0),
                              stop=(t == NT - 1))
                last.then_inc(S["grad_ps"], 1)
            pe.wait_ge(S["nws_ready"], 1)
            mm(P[0:D, 0, 0:D], wq_t[:], nws[0:D, 0, :], start=True, stop=True).then_inc(S["wz_ps"], 1)
            pe.wait_ge(S["wqproj_ready"], 1)
            pe.wait_ge(S["weights_split"], 1)
            pe.sem_inc(S["x1_free"], 1)
            with pe.Fori(0, IMAGES) as i:
                pe.wait_ge(S["x1_back"], 16 * i + 16)
                transposes(lambda t: x1[:, t, :], D, 0, S["pre_ps"])
                pe.wait_ge(S["ar_ready"], 4 * i + 2)
                pe.sem_inc(S["x1_free"], 1)
                for t in range(NT):
                    last = mm(flat[0:TP, 2 * BANK + t * 128:2 * BANK + t * 128 + 128], xt[:, t * TP:(t + 1) * TP],
                              wqproj[:], start=True, stop=True)
                last.then_inc(S["pre_ps"], 1)
                pe.wait_ge(S["a1_used"], i + 1)
                transposes(lambda t: a1[:, t, 0:D], D, 4, S["pre_ps"])
                pe.wait_ge(S["ar_ready"], 4 * i + 4)
                for t in range(NT):
                    last = mm(P[0:TP, 6, t * D:(t + 1) * D], at[:, t * TP:(t + 1) * TP], nws[:, 1, :],
                              start=True, stop=True)
                last.then_inc(S["pre_ps"], 1)
                pe.wait_ge(S["xd_ready"], 2 * i + 1)
                transposes(lambda t: xd[:, t, :, :].rearrange("p a f -> p (a f)"), 128, 0, S["xd_ps"])
                pe.wait_ge(S["xs_ready"], 4 * i + 2)
                for c in range(2):
                    for k in range(2):
                        for w in (wah, wal):
                            last = mm(P[0:QK, 2 + 2 * k + c, 0:width(c)], w[:, k * QK:(k + 1) * QK],
                                      xs[:, tok_cols(c)], start=(w is wah), stop=(w is wal))
                    last.then_inc(S["qk_ps"], 1)
                for t in range(NT):
                    for w in (wah, wal):
                        last = mm(P[0:TP, 6, t * 32:(t + 1) * 32], xs[:, t * TP:(t + 1) * TP], w[:, 2 * QK:],
                                  start=(w is wah), stop=(w is wal))
                last.then_inc(S["qk_ps"], 1)
                pe.wait_ge(S["qkl_ready"], i + 1)
                for o in range(3):
                    for c in range(2):
                        n = 2 * o + c
                        if n >= 4:
                            pe.wait_ge(S["qx_saved"], 6 * i + n - 3)
                        b = n % 4
                        mm(P[:, b, 0:width(c)], sel[0:QK, o, :], qkh[:, tok_cols(c)], start=True, stop=False)
                        mm(P[:, b, 0:width(c)], sel[0:QK, 3 + o, :], qkl[:, tok_cols(c)], start=False,
                           stop=True).then_inc(S["spread_ps"], 1)
                pe.wait_ge(S["qx_saved"], 6 * i + 6)
                pe.wait_ge(S["qx_zero"], i + 1)
                for qt in range(NT):
                    for h in range(NH):
                        n = qt * NH + h
                        if n >= 4:
                            pe.wait_ge(S["smax_read"], 28 * i + n - 3)
                        o = (n % 4) * 2 * BANK
                        keys = (qt + 1) * TP
                        for k0 in range(0, keys, BANK):
                            k1 = min(keys, k0 + BANK)
                            diag = max(k0, qt * TP)
                            mm(flat[0:TP, o + k0:o + k1], qx[:, h, qt * TP:keys], kx[:, h // 2, k0:k1],
                               start=True, stop=diag >= k1)
                            if diag < k1:
                                last = mm(flat[0:TP, o + diag:o + k1], idb[:],
                                          maskb[:, diag - qt * TP:k1 - qt * TP], start=False, stop=True)
                        last.then_inc(S["smax_ps"], 1)
                pe.wait_ge(S["mx_ready"], 28 * i + 28)
                for c, (t0, t1) in enumerate(CHUNKS):
                    for t in range(t0, t1):
                        last = mm(P[64:96, c, (t - t0) * TP:(t - t0 + 1) * TP], mx[:, t, :], ident[0:TP, 0:TP],
                                  start=True, stop=True)
                    last.then_inc(S["mxt_ps"], 1)
                pe.wait_ge(S["mrow_act"], 4 * i + 4)
                pe.wait_ge(S["mrow_dve"], 4 * i + 4)

                def scores(n):
                    kb, q0, q1 = PIECES[n]
                    for hp in range(2):
                        m = 2 * n + hp
                        if m >= 3:
                            pe.wait_ge(S["exp_done"], 22 * i + m - 2)
                        for j in range(2):
                            last = mm(P[0:TP, (m % 3) * 2 + j, 0:q1 - q0], kx[:, hp, kb * TP:(kb + 1) * TP],
                                      qx[:, 2 * hp + j, q0:q1], start=True, stop=True)
                        last.then_inc(S["st_ps"], 1)

                def values(n):
                    kb, q0, q1 = PIECES[n]
                    pe.wait_ge(S["exp_done"], 22 * i + 2 * n + 2)
                    if q0 == kb * TP:
                        pe.wait_ge(S["diag_done"], 14 * i + 2 * kb + 2)
                    c = q0 >= 448
                    for h in range(NH):
                        last = mm(P[32 * h:32 * h + 32, 6 + c, q0 - 448 * c:q1 - 448 * c], v1[:, kb, h // 2, :],
                                  pt[0:TP, kb % 2, h, q0:q1], start=(kb == 0), stop=(kb == (6 if c else 3)))
                    last.then_inc(S["pv_ps"], 1)

                for n in range(len(PIECES) + 1):
                    if n < len(PIECES):
                        scores(n)
                    if n:
                        values(n - 1)
                for c in range(2):
                    pe.wait_ge(S["pv_saved"], 2 * i + c + 1)
                    mm(P[:, c, 0:width(c)], con[:, C_DEN:C_DEN + 128], pv[:, tok_cols(c)], start=True,
                       stop=True).then_inc(S["den_ps"], 1)
                pe.wait_ge(S["yn_ready"], i + 1)
                for t in range(NT):
                    last = mm(P[0:TP, 2, t * D:(t + 1) * D], yn[:, t * TP:(t + 1) * TP], wo[:], start=True,
                              stop=True)
                last.then_inc(S["wo_ps"], 1)
                pe.wait_ge(S["xd_ready"], 2 * i + 2)
                transposes(lambda t: xd[:, t, :, :].rearrange("p a f -> p (a f)"), 128, 0, S["xd_ps"])
                pe.wait_ge(S["xs_ready"], 4 * i + 4)
                for t in range(NT):
                    for w in (wrh, wrl):
                        last = mm(P[0:TP, 3, t * NE:(t + 1) * NE], xs[:, t * TP:(t + 1) * TP], w[:],
                                  start=(w is wrh), stop=(w is wrl))
                last.then_inc(S["logit_ps"], 1)
                pe.wait_ge(S["wt_ready"], i + 1)
                transposes(lambda t: wt[:, t, :], 40, 0, S["wt_ps"])
                pe.wait_ge(S["wts_ready"], 2 * i + 2)
                def up(n):
                    c, p, k = n // 12, n // 3 % 4, n % 3
                    w0 = p * PAIR_W + k * MAIN
                    m = TAIL_W if k == 2 else MAIN
                    for j, (b, ready, freed) in enumerate(((0, "h1_ps", "silu_done"), (3, "h3_ps", "hh_ready"))):
                        if n >= 3:
                            pe.wait_ge(S[freed], 24 * i + n - 2)
                        o = w0 + j * PAIRS * PAIR_W
                        for w in (wmh, wml):
                            last = mm(P[0:m, b + n % 3, 0:width(c)], w[:, o:o + m], xs[:, tok_cols(c)],
                                      start=(w is wmh), stop=(w is wml))
                        last.then_inc(S[ready], 1)

                def down(g):
                    c, p = g // 4, g % 4
                    w = width(c)
                    if g >= 1:
                        pe.wait_ge(S["bw_saved"], 8 * i + g)
                    mm(P[:, 6, 0:w], selp[:, p, :], wts[:, tok_cols(c)], start=True,
                       stop=True).then_inc(S["bw_ps"], 1)
                    pe.wait_ge(S["hh_ready"], 24 * i + 3 * g + 3)
                    if g >= 1:
                        pe.wait_ge(S["z_ready"], 8 * i + g)
                    for e in range(2):
                        mm(P[64 * e:64 * e + 64, 7, 0:w], w2[:, 3 * p + e, :], hh[:, e, 0:w], start=True,
                           stop=False)
                    for e in range(2):
                        last = mm(P[64 * e:64 * e + 64, 7, 0:w], w2[64 * e:64 * e + TAIL, 3 * p + 2, :],
                                  hh[64 * e:64 * e + TAIL, 2, 0:w], start=False, stop=True)
                    last.then_inc(S["y_ps"], 1)

                for n in range(24):
                    up(n)
                    if n % 3 == 2:
                        down(n // 3)
                pe.wait_ge(S["z_added"], 8 * i + 8)
                for t in range(NT):
                    last = mm(P[0:TP, 0, t * D:(t + 1) * D], zacc[:, t * TP:(t + 1) * TP],
                              con[:, C_FOLD:C_FOLD + 64], start=True, stop=True)
                last.then_inc(S["fold_ps"], 1)

        @block.scalar
        def _(act):
            copy = lambda out, in_: nc.scalar.activation(out, in_, ACT.Copy)

            def evacuate(dst, rows, b, ps, ready, i, per, n):
                for c in range(2):
                    act.wait_ge(S[ps], i * per + n + c)
                    copy(dst[0:rows, tok_cols(c)], P[0:rows, b + c, 0:width(c)]).then_inc(S[ready], 1)

            act.wait_ge(S["set_done"], 1)
            with act.Fori(0, IMAGES) as i:
                act.wait_ge(S["h_ps"], i + 1)
                copy(h_all[:, bass.ds(i * NT * D, NT * D)], P[0:TP, 0, 0:NT * D]).then_inc(S["h_saved"], 1)
                evacuate(xt, D, 1, "xt_ps", "xt_ready", i, 6, 1)
                act.wait_ge(S["proj_ps"], i + 1)
                pr = flat[0:TP, 3 * BANK:3 * BANK + NT * 256].rearrange("p (t f) -> p t f", f=256)
                nc.scalar.activation(sg[:], pr[:, :, 0:D], ACT.Sigmoid).then_inc(S["sig1"], 1)
                copy(ke[:, :, 0:D], pr[:, :, D:2 * D]).then_inc(S["keys_saved"], 1)
                nc.scalar.activation(st[:, 4, :], pr[:, :, 192], ACT.Sigmoid).then_inc(S["alr_ready"], 1)
                evacuate(at, D, 1, "xt_ps", "xt_ready", i, 6, 3)
                act.wait_ge(S["z2_ps"], i + 1)
                act.wait_ge(S["slope1_ready"], i + 1)
                nc.scalar.activation(sg[:], tiles(0), ACT.Sigmoid).then_inc(S["sig2"], 1)
                evacuate(xt, D, 1, "xt_ps", "xt_ready", i, 6, 5)
            with act.Fori(0, IMAGES) as i:
                evacuate(xt, D, 0, "pre_ps", "ar_ready", i, 6, 1)
                act.wait_ge(S["pre_ps"], 6 * i + 3)
                zq = flat[0:TP, 2 * BANK:2 * BANK + NT * 128].rearrange("p (t f) -> p t f", f=128)
                nc.scalar.activation(sg[:], zq[:, :, 0:D], ACT.Silu).then_inc(S["silu_z"], 1)
                evacuate(at, D, 4, "pre_ps", "ar_ready", i, 6, 4)
                act.wait_ge(S["pre_ps"], 6 * i + 6)
                nc.scalar.activation(sq[:], tiles(6), ACT.Silu).then_inc(S["silu_z2"], 1)
                evacuate(xh, 128, 0, "xd_ps", "xh_ready", i, 4, 1)
                act.wait_ge(S["qk_ps"], 3 * i + 3)
                v = P[0:TP, 6, 0:NT * 32].rearrange("p (t g d) -> p t g d", g=NKV, d=HD)
                for g in range(NKV):
                    last = copy(v1[:, :, g, 0:HD], v[:, :, g, :])
                last.then_inc(S["v_saved"], 1)
                act.wait_ge(S["rope_done"], i + 1)
                copy(qkh[:], qk[:]).then_inc(S["qkh_ready"], 1)
                for o in range(3):
                    for c in range(2):
                        act.wait_ge(S["spread_ps"], 6 * i + 2 * o + c + 1)
                        dst = kx if o == 2 else qx
                        first = 0 if o == 2 else 2 * o
                        b = (2 * o + c) % 4
                        copy(dst[0:64, first, tok_cols(c)], P[0:64, b, 0:width(c)])
                        copy(dst[0:64, first + 1, tok_cols(c)],
                             P[64:128, b, 0:width(c)]).then_inc(S["qx_saved"], 1)
                for c in range(2):
                    act.wait_ge(S["mxt_ps"], 2 * i + 2)
                    for h in range(2):
                        nc.scalar.activation(qx[64:96, h, tok_cols(c)], P[64:96, c, 0:width(c)], ACT.Copy,
                                             scale=con[64:96, C_MAXROW + h:C_MAXROW + h + 1]
                                             ).then_inc(S["mrow_act"], 1)
                for n, (kb, q0, q1) in enumerate(PIECES):
                    for hp in range(2):
                        m = 2 * n + hp
                        act.wait_ge(S["st_ps"], 22 * i + m + 1)
                        if kb >= 2:
                            act.wait_ge(S["pv_ps"], 11 * i + first_piece(kb - 1))
                        b = (m % 3) * 2
                        nc.scalar.activation(pt[0:TP, kb % 2, 2 * hp:2 * hp + 2, q0:q1], P[0:TP, b:b + 2, 0:q1 - q0],
                                             ACT.Exp, scale=float(HD) ** -0.5).then_inc(S["exp_done"], 1)
                act.wait_ge(S["pv_ps"], 11 * i + 11)
                for c in range(2):
                    copy(pv[:, tok_cols(c)], P[:, 6 + c, 0:width(c)]).then_inc(S["pv_saved"], 1)
                evacuate(xh, 128, 0, "xd_ps", "xh_ready", i, 4, 3)
                act.wait_ge(S["logit_read"], i + 1)
                nc.scalar.activation(rt[:, 1, :, :], rt[:, 0, :, :], ACT.Exp).then_inc(S["exp_r"], 1)
                evacuate(wth, 40, 0, "wt_ps", "wth_ready", i, 2, 1)
                for n in range(24):
                    c = n // 12
                    w = width(c)
                    act.wait_ge(S["h1_ps"], 24 * i + n + 1)
                    if n >= 2:
                        act.wait_ge(S["hh_ready"], 24 * i + n - 1)
                    nc.scalar.activation(su[:, n % 2, 0:w], P[:, n % 3, 0:w], ACT.Silu).then_inc(S["silu_done"], 1) \
                        if n % 3 < 2 else \
                        nc.scalar.activation(su[0:TAIL_W, n % 2, 0:w], P[0:TAIL_W, n % 3, 0:w],
                                             ACT.Silu).then_inc(S["silu_done"], 1)
                    if n % 3 == 2:
                        g = n // 3
                        act.wait_ge(S["bw_ps"], 8 * i + g + 1)
                        if g >= 2:
                            act.wait_ge(S["z_ready"], 8 * i + g - 1)
                        copy(bw[:, g % 2, 0:w], P[:, 6, 0:w]).then_inc(S["bw_saved"], 1)

        @block.vector
        def _(dve):
            V = nc.vector
            chain = Steps(dve, S["dve_steps"])
            link = chain.link

            def over_tiles(s, n=D):
                return s.unsqueeze(2).broadcast_to([TP, NT, n])

            def mean_rstd(src, centre, var, rstd, n):
                if centre:
                    link(V.reduce_sum(st[:, 0, :], src, axis=AX.X))
                    link(V.tensor_scalar(st[:, 1, :], st[:, 0, :], 1.0 / D, None, ALU.mult))
                    link(V.tensor_tensor(xc[:], src, over_tiles(st[:, 1, :]), ALU.subtract))
                    src = xc[:]
                link(V.tensor_tensor(sq[:], src, src, ALU.mult))
                link(V.reduce_sum(st[:, 5, :], sq[:], axis=AX.X))
                V.tensor_scalar(st[:, 2, :], st[:, 5, :], 1.0 / D, EPS_LN if centre else EPS_RMS, ALU.mult,
                                ALU.add).then_inc(var, 1)
                dve.wait_ge(rstd, n)

            dve.wait_ge(S["loaded"], 16 * N_LOADS)
            dve.wait_ge(S["set_done"], 1)
            V.tensor_copy(sel[:], con[:, C_SELH:C_SELH + 768].rearrange("p (o r) -> p o r", o=6))
            V.tensor_copy(selp[:], con[0:40, C_PAIR:C_PAIR + PAIRS * 128].rearrange("p (o r) -> p o r", o=PAIRS))
            V.tensor_copy(idb[:], con[0:TP, C_ID:C_ID + TP])
            V.tensor_copy(maskb[:], con[0:TP, C_MASK:C_MASK + TP])
            for raw, hi, lo, ln in ((araw, wah, wal, 0), (rraw, wrh, wrl, 1), (mraw, wmh, wml, 1)):
                link(V.tensor_scalar(raw[:], raw[:], lnw[:, ln:ln + 1], None, ALU.mult))
                link(V.tensor_copy(hi[:], raw[:]))
                last = V.tensor_tensor(lo[:], raw[:], hi[:].bitcast(F32), ALU.subtract)
            last.then_inc(S["weights_split"], 1)
            dve.wait_ge(S["wz0_ps"], 1)
            V.tensor_copy(wproj[0:D, 0:D], P[0:D, 0, 0:D])
            V.tensor_copy(wproj[D:D + 1, 0:D], ws[D:D + 1, 0, :]).then_inc(S["wproj_ready"], 1)
            dve.sem_inc(S["patch_used"], 1)
            dve.sem_inc(S["x1_stored"], 16)
            dve.sem_inc(S["out_sent"], 16)
            with dve.Fori(0, IMAGES) as i:
                chain.loop(i, D1)
                dve.wait_ge(S["h_saved"], i + 1)
                dve.sem_inc(S["patch_used"], 1)
                h = h_all[:, bass.ds(i * NT * D, NT * D)].rearrange("p (t f) -> p t f", f=D)
                mean_rstd(h, True, S["var_ready"], S["rstd_ready"], i + 1)
                dve.wait_ge(S["x1_stored"], 16 * i + 16)
                V.tensor_tensor(x1[:], xc[:], over_tiles(st[:, 3, :]), ALU.mult).then_inc(S["x1_ready"], 1)
                pr = flat[0:TP, 3 * BANK:3 * BANK + NT * 256].rearrange("p (t f) -> p t f", f=256)
                dve.wait_ge(S["alr_ready"], i + 1)
                V.tensor_tensor(si[:], pr[:, :, 0:D], sg[:], ALU.mult).then_inc(S["si1_ready"], 1)
                dve.wait_ge(S["si1_ready"], i + 1)
                V.tensor_tensor(a1[:, :, 0:D], ke[:, :, 0:D], si[:], ALU.add).then_inc(S["a1_ready"], 1)
                dve.wait_ge(S["a1_ready"], i + 1)
                V.tensor_tensor(xc[:], a1[:, :, 0:D], pr[:, :, 2 * D:3 * D], ALU.subtract)
                link(V.tensor_scalar(st[:, 6, :], st[:, 4, :], MAX_ALR * 2.0 / D, None, ALU.mult))
                dve.wait_ge(S["sig2"], i + 1)
                V.tensor_tensor(si[:], tiles(0), sg[:], ALU.mult).then_inc(S["si2_ready"], 1)
                dve.wait_ge(S["si2_ready"], i + 1)
                link(V.tensor_tensor(xc[:], xc[:], si[:], ALU.add))
                link(V.tensor_tensor(dp[:], xc[:], over_tiles(st[:, 6, :]), ALU.mult))
                dve.wait_ge(S["slope2_ready"], i + 1)
                V.tensor_tensor(dz[:], dp[:], sp2[:], ALU.mult).then_inc(S["dz2_ready"], 1)
                dve.wait_ge(S["da_ps"], i + 1)
                link(V.tensor_tensor(xc[:], tiles(0), dp[:], ALU.add))
                V.tensor_tensor(dz1[:], xc[:], sp1[:], ALU.mult).then_inc(S["dz1_ready"], 1)
                dve.wait_ge(S["grad_ps"], i + 1)
                V.tensor_tensor(gacc[:], gacc[:], P[0:D + 1, 7, 0:2 * D].rearrange("p (l n) -> p l n", l=2),
                                ALU.add).then_inc(S["grads_summed"], 1)
            chain.unloop(IMAGES)
            dve.wait_ge(S["grads_summed"], IMAGES)
            link(V.tensor_scalar(gtmp[:], gacc[:], -1.0, None, ALU.mult))
            link(V.tensor_tensor(gtmp[:], gacc[:], gtmp[:], ALU.max))
            link(V.tensor_scalar(gtmp[:], gtmp[:], EPS_ADAM, None, ALU.add))
            link(V.reciprocal(gtmp[:], gtmp[:]))
            link(V.tensor_tensor(gtmp[:], gacc[:], gtmp[:], ALU.mult))
            link(V.tensor_scalar(gtmp[:], gtmp[:], LR, None, ALU.mult))
            link(V.tensor_scalar(nws[:], ws[:], 1.0 - LR * WD, None, ALU.mult))
            V.tensor_tensor(nws[:], nws[:], gtmp[:], ALU.subtract).then_inc(S["nws_ready"], 1)
            dve.wait_ge(S["nws_ready"], 1)
            dve.wait_ge(S["wz_ps"], 1)
            V.tensor_copy(wqproj[0:D, 0:D], P[0:D, 0, 0:D])
            V.tensor_copy(wqproj[D:D + 1, 0:D], nws[D:D + 1, 0, :]).then_inc(S["wqproj_ready"], 1)
            rs = lambda k: rt[:, k, :, :]
            with dve.Fori(0, IMAGES) as i:
                chain.loop(i, D2)
                zq = flat[0:TP, 2 * BANK:2 * BANK + NT * 128].rearrange("p (t f) -> p t f", f=128)
                dve.wait_ge(S["silu_z"], i + 1)
                V.tensor_tensor(a1[:, :, 0:D], zq[:, :, D:], sg[:], ALU.add).then_inc(S["a1_used"], 1)
                dve.wait_ge(S["a1_used"], i + 1)
                link(V.tensor_tensor(h2[:], a1[:, :, 0:D],
                                     h_all[:, bass.ds(i * NT * D, NT * D)].rearrange("p (t f) -> p t f", f=D),
                                     ALU.add))
                dve.wait_ge(S["silu_z2"], i + 1)
                link(V.tensor_tensor(h2[:], h2[:], sq[:], ALU.add))
                mean_rstd(h2[:], True, S["q_var"], S["q_rstd"], 3 * i + 1)
                link(V.tensor_tensor(x2[:], xc[:], over_tiles(st[:, 3, :]), ALU.mult))

                def normed(src, k):
                    mean_rstd(src, False, S["q_var"], S["q_rstd"], 3 * i + 2 + k)
                    V.tensor_tensor(xd[:], src.unsqueeze(2).broadcast_to([TP, NT, 2, D]),
                                    st[:, 3, :].unsqueeze(2).unsqueeze(3).broadcast_to([TP, NT, 2, D]),
                                    ALU.mult).then_inc(S["xd_ready"], 1)
                    for c in range(2):
                        dve.wait_ge(S["xh_ready"], 4 * i + 2 * k + c + 1)
                        V.scalar_tensor_tensor(xs[:, tok_cols(c)], xh[:, tok_cols(c)].bitcast(F32),
                                               con[:, C_LOW64:C_LOW64 + 1], P[:, c, 0:width(c)], ALU.mult,
                                               ALU.add).then_inc(S["xs_ready"], 1)

                normed(x2[:], 0)
                for c in range(2):
                    dve.wait_ge(S["qk_ps"], 3 * i + c + 1)
                    V.tensor_tensor(qk[:, tok_cols(c)], P[0:QK, 2 + c, 0:width(c)], rope[:, 0, tok_cols(c)], ALU.mult)
                    link(V.tensor_tensor(qk_sin[:, tok_cols(c)], P[0:QK, 4 + c, 0:width(c)], rope[:, 1, tok_cols(c)],
                                         ALU.mult))
                V.tensor_tensor(qk[:], qk[:], qk_sin[:], ALU.add).then_inc(S["rope_done"], 1)
                dve.wait_ge(S["qkh_ready"], i + 1)
                V.tensor_tensor(qkl[:], qk[:], qkh[:].bitcast(F32), ALU.subtract).then_inc(S["qkl_ready"], 1)
                for qt in range(NT):
                    for h in range(NH):
                        n = qt * NH + h
                        dve.wait_ge(S["smax_ps"], 28 * i + n + 1)
                        o = (n % 4) * 2 * BANK
                        V.reduce_max(mx[:, qt, h:h + 1], flat[0:TP, o:o + (qt + 1) * TP],
                                     axis=AX.X).then_inc(S["smax_read"], 1)
                dve.wait_ge(S["smax_read"], 28 * i + 28)
                dve.sem_inc(S["mx_ready"], 28)
                dve.wait_ge(S["mrow_act"], 4 * i + 4)
                for c in range(2):
                    for h in range(2, NH):
                        V.tensor_scalar(qx[64:96, h, tok_cols(c)], P[64:96, c, 0:width(c)],
                                        con[64:96, C_MAXROW + h:C_MAXROW + h + 1], None,
                                        ALU.mult).then_inc(S["mrow_dve"], 1)
                for c in range(2):
                    dve.wait_ge(S["den_ps"], 2 * i + c + 1)
                    ins = V.reciprocal(rden[:, tok_cols(c)], P[:, c, 0:width(c)])
                ins.then_inc(S["rden_ready"], 1)
                dve.wait_ge(S["wo_ps"], i + 1)
                link(V.tensor_tensor(x2[:], x2[:], tiles(2), ALU.add))
                V.tensor_tensor(h2[:], h2[:], x2[:], ALU.add)
                normed(x2[:], 1)
                dve.wait_ge(S["logit_ps"], i + 1)
                lg = P[0:TP, 3, 0:NT * NE].rearrange("p (t e) -> p t e", e=NE)
                link(V.reduce_max(st[:, 0, :], lg, axis=AX.X))
                V.tensor_tensor(rs(0), lg, over_tiles(st[:, 0, :], NE), ALU.subtract).then_inc(S["logit_read"], 1)
                dve.wait_ge(S["exp_r"], i + 1)
                link(V.reduce_sum(st[:, 1, :], rs(1), axis=AX.X))
                link(V.reciprocal(st[:, 1, :], st[:, 1, :]))
                link(V.tensor_tensor(rs(1), rs(1), over_tiles(st[:, 1, :], NE), ALU.mult))
                link(V.tensor_copy(rs(2), rs(1)))
                link(V.memset(rs(6), 0.0))
                rank = con[0:TP, C_RANK:C_RANK + NT * NE].rearrange("p (t e) -> p t e", e=NE)
                for k in range(2):
                    link(V.reduce_max(st[:, 4 + k, :], rs(2), axis=AX.X))
                    link(V.tensor_tensor(rs(3), rs(2), over_tiles(st[:, 4 + k, :], NE), ALU.is_equal))
                    link(V.tensor_tensor(rs(3), rs(3), rank, ALU.mult))
                    link(V.reduce_max(st[:, 6, :], rs(3), axis=AX.X))
                    link(V.tensor_tensor(rs(4), rank, over_tiles(st[:, 6, :], NE), ALU.is_equal))
                    link(V.tensor_tensor(rs(6), rs(6), rs(4), ALU.add))
                    if k == 0:
                        link(V.scalar_tensor_tensor(rs(2), rs(4), -2.0, rs(2), ALU.mult, ALU.add))
                link(V.tensor_tensor(rs(1), rs(1), rs(6), ALU.mult))
                link(V.reduce_sum(st[:, 6, :], rs(1), axis=AX.X))
                link(V.tensor_scalar(st[:, 6, :], st[:, 6, :], EPS_TOP, None, ALU.add))
                link(V.reciprocal(st[:, 6, :], st[:, 6, :]))
                link(V.tensor_tensor(wt[:, :, 0:NE], rs(1), over_tiles(st[:, 6, :], NE), ALU.mult))
                V.tensor_copy(wt[:, :, 32:40], wt[:, :, 0:NE]).then_inc(S["wt_ready"], 1)
                for c in range(2):
                    dve.wait_ge(S["wth_ready"], 2 * i + c + 1)
                    V.scalar_tensor_tensor(wts[:, tok_cols(c)], wth[:, tok_cols(c)].bitcast(F32),
                                           con[0:40, C_LOW32:C_LOW32 + 1], P[0:40, c, 0:width(c)], ALU.mult,
                                           ALU.add).then_inc(S["wts_ready"], 1)
                for n in range(24):
                    c = n // 12
                    w = width(c)
                    r = TAIL_W if n % 3 == 2 else 128
                    dve.wait_ge(S["silu_done"], 24 * i + n + 1)
                    dve.wait_ge(S["h3_ps"], 24 * i + n + 1)
                    if n >= 3:
                        dve.wait_ge(S["y_ps"], 8 * i + n // 3)
                    V.tensor_tensor(hh[0:r, n % 3, 0:w], su[0:r, n % 2, 0:w], P[0:r, 3 + n % 3, 0:w],
                                    ALU.mult).then_inc(S["hh_ready"], 1)
                    if n % 3 == 2:
                        g = n // 3
                        dve.wait_ge(S["y_ps"], 8 * i + g + 1)
                        dve.wait_ge(S["bw_saved"], 8 * i + g + 1)
                        if g >= 2:
                            dve.wait_ge(S["z_added"], 8 * i + g - 1)
                        V.tensor_tensor(zz[:, g % 2, 0:w], bw[:, g % 2, 0:w], P[:, 7, 0:w],
                                        ALU.mult).then_inc(S["z_ready"], 1)
                dve.wait_ge(S["fold_ps"], i + 1)
                dve.wait_ge(S["out_sent"], i * 16 + 16)
                V.tensor_tensor(res[:], h2[:], tiles(0), ALU.add).then_inc(S["out_ready"], 1)
            chain.unloop(IMAGES)


PIECES = [(kb, q0, q1) for kb in range(NT)
          for q0, q1 in (((kb * TP, 448), (448, TOK)) if kb < 4 else ((kb * TP, TOK),))]


def first_piece(kb):
    return next(n for n, p in enumerate(PIECES) if p[0] == kb)


def lay_out(x, L0_tok_W, L0_tok_b, L0_attn_Wk, L0_attn_Wq, L0_attn_Wv, L0_attn_Wlr, L0_attn_blr, L0_attn_Ws,
            L0_attn_bs, L0_ffn_ln1_w, L0_ffn_ln2_w, L0_ffn_wq, L0_ffn_wk, L0_ffn_wv, L0_ffn_wo, L0_ffn_router_w,
            L0_ffn_w1, L0_ffn_w2, L0_ffn_w3):
    n = SIDE
    patches = x.reshape(IMAGES, n, PATCH, n, PATCH).transpose(2, 4, 0, 1, 3).reshape(D, IMAGES * TOK)
    col = lambda a: a.reshape(1, -1)
    zero = lambda *s: np.zeros(s, np.float32)
    wproj = np.concatenate([
        np.concatenate([L0_attn_Wk, L0_attn_Wv, L0_attn_Wlr], 1),
        np.concatenate([zero(1, 2 * D), col(L0_attn_blr)], 1)], 0)
    half = HD // 2
    swap = (np.arange(QK) // HD) * HD + (np.arange(QK) % HD + half) % HD
    wqk = np.concatenate([L0_ffn_wq, L0_ffn_wk], 0)
    attnw = np.concatenate([wqk, wqk[swap], L0_ffn_wv], 0).T
    pairs = []
    for w in (L0_ffn_w1, L0_ffn_w3):
        for p in range(PAIRS):
            e, f = w[2 * p], w[2 * p + 1]
            pairs += [e[:MAIN], f[:MAIN], e[MAIN:], zero(64 - TAIL, D), f[MAIN:]]
    w13 = np.concatenate(pairs, 0).T
    w2 = zero(128, 3 * PAIRS, D)
    for p in range(PAIRS):
        for k in range(2):
            t = L0_ffn_w2[2 * p + k].T
            w2[:, 3 * p + k] = t[:MAIN]
            w2[64 * k:64 * k + TAIL, 3 * p + 2] = t[MAIN:]
    wo = zero(128, D)
    for h in range(NH):
        wo[32 * h:32 * h + HD] = L0_ffn_wo[:, h * HD:(h + 1) * HD].T
    con, rope = shape_constants()
    out = {
        "con": con, "rope": rope, "patches": patches,
        "tokw": np.concatenate([L0_tok_W.T, col(L0_tok_b)], 0),
        "wk_t": L0_attn_Wk.T, "wq_t": L0_attn_Wq.T, "w1l_t": L0_attn_Ws[1].T,
        "ws": np.concatenate([L0_attn_Ws.transpose(1, 0, 2), L0_attn_bs[None]], 0),
        "wproj": wproj, "wqp": np.concatenate([L0_attn_Wq, zero(1, D)], 0),
        "attnw": attnw, "router": L0_ffn_router_w.T, "lnw": np.stack([L0_ffn_ln1_w, L0_ffn_ln2_w], 1),
        "w13": w13, "w2": w2, "wo": wo,
    }
    return {k: np.ascontiguousarray(v) for k, v in out.items()}


def kernel(**inputs):
    import concourse.bacc as bacc
    from concourse.bass_utils import run_bass_kernel_spmd

    arrays = lay_out(**{k: np.asarray(v) for k, v in inputs.items()})
    nc = bacc.Bacc("TRN2", target_bir_lowering=False, num_devices=1)
    aps = {k: nc.dram_tensor(f"in_{k}", v.shape, F32, kind="ExternalInput").ap() for k, v in arrays.items()}
    out = nc.dram_tensor("out_tokens", (IMAGES * TOK, D), F32, kind="ExternalOutput").ap()
    aps["out"] = out.rearrange("(t p) f -> p t f", p=TP)
    vit_block(nc, aps)
    r = run_bass_kernel_spmd(nc, [{f"in_{k}": v for k, v in arrays.items()}], core_ids=[0])
    return r.results[0]["out_tokens"].reshape(IMAGES, TOK, D)
```

```python
from contextlib import ExitStack

import numpy as np

import concourse.bass as bass
from concourse import mybir

F32 = mybir.dt.float32
F32R = mybir.dt.float32r
BF16 = mybir.dt.bfloat16
ALU = mybir.AluOpType
ACT = mybir.ActivationFunctionType
AX = mybir.AxisListType

IMAGES = 16
SIDE = 28
TOK = SIDE * SIDE
TP = 112
NT = TOK // TP
D = 64
PATCH = 8
NH, NKV, HD = 4, 2, 16
QK = (NH + NKV) * HD
NE, HID = 8, 170
PAIRS = NE // 2
MAIN = 128
TAIL = HID - MAIN
TAIL_W = 64 + TAIL
PAIR_W = 2 * MAIN + TAIL_W
CHUNKS = [(0, 4), (4, 7)]
BANK = 512
LR, WD, MAX_ALR, EPS_ADAM = 0.001, 0.01, 0.1, 1e-8
EPS_LN, EPS_RMS, EPS_TOP = 1e-5, 1e-6, 1e-9
NEG = -1e30
Q_ROWS = 96

C_ID = 0
C_MASK = C_ID + 128
C_SELH = C_MASK + TP
C_SELL = C_SELH + 3 * 128
C_PAIR = C_SELL + 3 * 128
C_DEN = C_PAIR + PAIRS * 128
C_FOLD = C_DEN + 128
C_LOW64 = C_FOLD + 64
C_LOW32 = C_LOW64 + 1
C_MAXROW = C_LOW32 + 1
C_RANK = C_MAXROW + NH
C_HALF = C_RANK + NT * NE
C_ALL = C_HALF + NT


def shape_constants():
    c = np.zeros((128, C_ALL), np.float32)
    c[:, C_ID:C_ID + 128] = np.eye(128)
    c[:TP, C_MASK:C_MASK + TP] = np.triu(np.full((TP, TP), NEG), 1)
    for out in range(3):
        for r in range(128):
            part, d = (r % 64) // 16, r % 16
            src = (out * 2 + r // 64) * HD + d
            low = part % 2 if out < 2 else part // 2
            c[src, (C_SELL if low else C_SELH) + out * 128 + r] = 1
    for p in range(PAIRS):
        for r in range(128):
            e = 2 * p + r // 64
            c[e, C_PAIR + p * 128 + r] = 1
            c[32 + e, C_PAIR + p * 128 + r] = 1
    for r in range(128):
        c[32 * (r // 32) + HD, C_DEN + r] = 1
    c[:, C_FOLD:C_FOLD + 64] = np.concatenate([np.eye(64), np.eye(64)])
    c[64:, C_LOW64] = -1
    c[32:64, C_LOW32] = -1
    for h in range(NH):
        c[64 + h, C_MAXROW + h] = -1
    c[:, C_RANK:C_RANK + NT * NE] = np.tile(np.arange(NE, 0, -1), NT)
    c[:, C_HALF:C_HALF + NT] = -0.5
    inv = 1.0 / 10000.0 ** (np.arange(0, HD, 2, dtype=np.float32) / HD)
    freqs = np.outer(np.arange(TOK, dtype=np.float32), inv)
    emb = np.concatenate([freqs, freqs], -1)
    sign = np.where(np.arange(HD) < HD // 2, -1, 1).astype(np.float32)
    cos = np.tile(np.cos(emb).T, (NH + NKV, 1))
    sin = np.tile((np.sin(emb) * sign).T, (NH + NKV, 1))
    return c, np.stack([cos, sin], 1).astype(np.float32)


class Image:

    def __init__(self, patch, hx_row, h, x1, xt, at, a1, ke, xc, sq, sg, si, sp1, sp2, dp, dz, dz1, st, bank):
        self.patch, self.hx_row, self.h, self.x1, self.xt, self.at = patch, hx_row, h, x1, xt, at
        self.a1, self.ke, self.xc, self.sq, self.sg, self.si = a1, ke, xc, sq, sg, si
        self.sp1, self.sp2, self.dp, self.dz, self.dz1, self.st = sp1, sp2, dp, dz, dz1, st
        self.bank = bank


class Steps:

    def __init__(self, eng, sem):
        self.eng, self.sem, self.start, self.n, self.base = eng, sem, 0, 0, 0

    def round(self, i, per):
        self.n, self.base = 0, self.start + i * per

    def link(self, ins):
        self.n += 1
        ins.then_inc(self.sem, 1)
        self.eng.wait_ge(self.sem, self.base + self.n)


def vit_block(nc, A):
    ctx = ExitStack()
    with ctx:
        def sb(name, shape, dt=F32):
            return ctx.enter_context(nc.sbuf_tensor(name, shape, dt))

        def sem(name):
            return ctx.enter_context(nc.semaphore(name))

        con = sb("con", [128, C_ALL])
        rope = sb("rope", [QK, 2, TOK])
        sel = sb("sel", [128, 6, 128], F32R)
        selp = sb("selp", [40, PAIRS, 128], F32R)
        idb = sb("idb", [TP, TP], BF16)
        maskb = sb("maskb", [TP, TP], BF16)
        ident = con[:, C_ID:C_ID + 128]
        tokw = sb("tokw", [D + 1, D])
        wk_t = sb("wk_t", [D, D])
        wq_t = sb("wq_t", [D, D])
        w1l_t = sb("w1l_t", [D, D])
        ws = sb("ws", [D + 1, 2, D])
        nws = sb("nws", [D + 1, 2, D])
        wproj = sb("wproj", [D + 1, 194])
        wqproj = sb("wqproj", [D + 1, 2 * D])
        NA = 2 * QK + NKV * HD
        NB = NE
        araw = sb("araw", [128, NA])
        wah = sb("wah", [128, NA], F32R)
        wal = sb("wal", [128, NA], F32R)
        rraw = sb("rraw", [128, NB])
        wrh = sb("wrh", [128, NB], F32R)
        wrl = sb("wrl", [128, NB], F32R)
        lnw = sb("lnw", [128, 2])
        wmh = sb("wmh", [128, 2 * PAIRS * PAIR_W], F32R)
        wml = sb("wml", [128, 2 * PAIRS * PAIR_W], F32R)
        w2 = sb("w2", [128, 3 * PAIRS, D])
        wo = sb("wo", [128, D])

        hx_store = nc.dram_tensor("hx_store", (TP, IMAGES, 2 * NT * D), F32, kind="Internal").ap()
        gacc = sb("gacc", [D + 1, 2, D])
        gtmp = sb("gtmp", [D + 1, 2, D])

        pv = sb("pv", [128, TOK])
        patch = pv[0:D + 1, :]
        hx = sb("hx", [TP, 2, NT, D])
        h_in, x1 = hx[:, 0, :, :], hx[:, 1, :, :]
        hx_row = hx[:].rearrange("p a t f -> p (a t f)")
        xt = sb("xt", [D + 1, TOK])
        at = sb("at", [D + 1, TOK])
        a1 = sb("a1", [TP, NT, D + 2])
        ke = sb("ke", [TP, NT, D + 2])
        tm = [sb(f"tm{n}", [TP, NT, D]) for n in range(6)]
        xc, sq, sg, si, sp1, sp2 = tm
        dp = sb("dp", [TP, NT, D])
        dz = sb("dz", [TP, NT, D])
        dz1 = sb("dz1", [TP, NT, D])
        st = sb("st", [TP, 8, NT])
        h2, x2, res = dp, dz1, dz
        h2_held, x2_held = sb("h2_held", [TP, NT, D]), sb("x2_held", [TP, NT, D])
        rest = sb("rest", [TP, NT, D])
        sq2 = sb("sq2", [TP, NT, D])
        st2 = sb("st2", [TP, 8, NT])
        xd2 = sb("xd2", [TP, NT, 2, D])
        xd = sb("xd", [TP, NT, 2, D])
        xh = sb("xh", [128, TOK], F32R)
        xs = sb("xs", [128, TOK], F32R)
        xm = sb("xm", [128, TOK], F32R)
        xmh = sb("xmh", [128, TOK], F32R)
        qk = sb("qk", [QK, TOK])
        qkh = sb("qkh", [QK, TOK], F32R)
        qkl = sb("qkl", [QK, TOK], F32R)
        qx = sb("qx", [Q_ROWS, NH, TOK], F32R)
        kx = sb("kx", [Q_ROWS, NKV, TOK], F32R)
        v1 = sb("v1", [TP, NT, NKV, 32])
        mx = sb("mx", [TP, NT, 32])
        pt = sb("pt", [128, 2, NH, TOK])
        mraw = pt[:].rearrange("p a h n -> p (a h n)")[:, 0:2 * PAIRS * PAIR_W]
        rden = sb("rden", [128, TOK])
        yn = sb("yn", [128, TOK])
        qk_sin = yn[0:QK, :]
        rt = sb("rt", [TP, 8, NT, NE])
        wt = sb("wt", [TP, NT, 40])
        wth = xmh[0:40, :]
        wts = sb("wts", [40, TOK], F32R)
        bw = sb("bw", [128, 2, 448])
        su = sb("su", [128, 2, 448])
        hh = sb("hh", [128, 2, 3, 448])
        zz = sb("zz", [128, 2, 448])
        zacc = sb("zacc", [128, TOK])

        rows = lambda buf, k: buf[0:TP, k, :].rearrange("p (t f) -> p t f", f=D)
        ext = lambda buf: buf[0:TP, 0:NT * (D + 2)].rearrange("p (t f) -> p t f", f=D + 2)
        hx_b = zz[0:TP].rearrange("p a n -> p (a n)")
        cols = lambda buf: buf[0:D + 1].rearrange("p t a f -> p (t a f)")[:, 0:TOK]
        IM = []
        for s in range(2):
            hid = [hh[0:TP, k // 3, k % 3, :].rearrange("p (t f) -> p t f", f=D) for k in range(6)]
            IM.append(Image(
                patch=(patch, yn[0:D + 1, :])[s], hx_row=(hx_row, hx_b)[s],
                h=(h_in, hx_b[:, 0:NT * D].rearrange("p (t f) -> p t f", f=D))[s],
                x1=(x1, hx_b[:, NT * D:].rearrange("p (t f) -> p t f", f=D))[s],
                xt=(xt[:], cols(xd))[s], at=(at[:], cols(xd2))[s],
                a1=(a1[:], ext(zacc))[s], ke=(ke[:], ext(rden))[s],
                xc=(xc[:], hid[0])[s], sq=(sq[:], hid[1])[s], sg=(sg[:], hid[2])[s], si=(si[:], hid[3])[s],
                sp1=(sp1[:], hid[4])[s], sp2=(sp2[:], hid[5])[s], dp=(dp[:], rows(su, 0))[s],
                dz=(dz[:], rows(su, 1))[s], dz1=(dz1[:], rows(bw, 0))[s], st=(st, st2)[s], bank=4 * s))

        P = ctx.enter_context(nc.psum_tensor("P", [128, 8, BANK], F32))
        flat = P[:, :, :].rearrange("p b n -> p (b n)")

        def tiles(b):
            return P[0:TP, b, 0:NT * D].rearrange("p (t f) -> p t f", f=D)

        def tok_cols(c):
            t0, t1 = CHUNKS[c]
            return slice(t0 * TP, t1 * TP)

        def width(c):
            return (CHUNKS[c][1] - CHUNKS[c][0]) * TP

        def spread_rows(copy, o, c):
            dst, first, b = kx if o == 2 else qx, 0 if o == 2 else 2 * o, (2 * o + c) % 4
            copy(dst[0:64, first, tok_cols(c)], P[0:64, b, 0:width(c)])
            return copy(dst[0:64, first + 1, tok_cols(c)], P[64:128, b, 0:width(c)])

        def in_turn(*stages):
            order, stages = stages[0], list(stages[1:])
            for which in order:
                next(stages[which], None)
            for stage in stages:
                for _ in stage:
                    pass

        def second_pass(eng, before, maxima, scores, after, experts):
            experts_and_maxima = [0, 1] * 28
            after_and_before = [0, 1, 1, 0, 1, 0, 1, 1, 0, 1, 0, 1, 0, 1, 0, 1]

            def round_(i, first=False, last=False):
                if first:
                    in_turn([], before(i))
                    in_turn([], maxima(i))
                else:
                    in_turn(experts_and_maxima, experts(i - 1), maxima(i))
                scores(i)
                if last:
                    in_turn([], after(i))
                    in_turn([], experts(i))
                else:
                    in_turn(after_and_before, after(i), before(i + 1))

            round_(0, first=True)
            with eng.Fori(1, IMAGES - 1) as i:
                round_(i)
            round_(IMAGES - 1, last=True)

        names = """loaded set_done weights_split wz0_ps wproj_ready dve_steps
            nws_ready wz_ps wqproj_ready hx_back hx_free pre_ps ar_ready a1_used
            xd_ready xd_ps xh_ready xs_ready qk_ps v_saved rope_done qkh_ready qkl_ready spread_ps qx_zero
            smax_ps smax_read mxt_ps mrow_act mrow_dve st_ps exp_done diag_done pv_ps pv_saved den_ps
            rden_ready yn_ready wo_ps logit_ps logit_read exp_r wt_ready wt_ps wth_ready wts_ready bw_ps
            bw_saved h1_ps h3_ps hh_ready y_ps z_ready z_added fold_ps out_ready out_sent
            pool_set waited tanh_z tanh_z2 rope_read rows_act rows_dve held post_steps pre_steps rest_ready
            rstd_post rstd_pre silu_done var_post var_pre xd2_ps xd2_ready xm_ready xmh_ready""".split()
        S = {n: sem(n) for n in names}
        in_first = """patch_in patch_used h_ps h_saved var_ready rstd_ready x1_ready hx_stored xt_ps xt_ready proj_ps
            sig1 keys_saved alr_ready si1_ready slope1_ready a1_ready values_read z2_ps sig2 si2_ready
            slope2_ready dz2_ready da_ps dz1_ready grad_ps dve_steps grads_summed pool_steps""".split()
        S1 = [{n: sem(f"{n}_{s}") for n in in_first} for s in range(2)]

        def first_pass(eng, image):
            with eng.Fori(0, IMAGES // 2) as r:
                in_turn([0, 1] * 9, image(r, 0), image(r, 1))

        block = ctx.enter_context(nc.Block())

        D1, D_PRE, D_POST = 9, 12, 24

        @block.sync
        def _(sp):
            for dst, src in ((con[:], A["con"]), (rope[:], A["rope"]), (tokw[:], A["tokw"]),
                             (wk_t[:], A["wk_t"]), (wq_t[:], A["wq_t"]), (w1l_t[:], A["w1l_t"]), (ws[:], A["ws"]),
                             (wproj[:, 64:193], A["wproj"]), (wqproj[:, D:], A["wqp"]),
                             (araw[0:64, :], A["attnw"]), (araw[64:128, :], A["attnw"]),
                             (rraw[0:64, :], A["router"]), (rraw[64:128, :], A["router"]),
                             (lnw[0:64, :], A["lnw"]), (lnw[64:128, :], A["lnw"]),
                             (mraw[0:64], A["w13"]), (mraw[64:128], A["w13"]),
                             (w2[:], A["w2"]), (wo[:], A["wo"])):
                sp.dma_start(dst, src).then_inc(S["loaded"], 16)
            with sp.Fori(0, IMAGES // 2) as r:
                for s in range(2):
                    sp.wait_ge(S1[s]["patch_used"], r + 1)
                    sp.dma_start(IM[s].patch[0:D, :],
                                 A["patches"][:, bass.ds((2 * r + s) * TOK, TOK)]).then_inc(S1[s]["patch_in"], 16)
                for s in range(2):
                    sp.wait_ge(S1[s]["x1_ready"], r + 1)
                    sp.dma_start(hx_store[:, bass.ds(2 * r + s, 1), :].rearrange("p a n -> p (a n)"),
                                 IM[s].hx_row).then_inc(S1[s]["hx_stored"], 16)
            for s in range(2):
                sp.wait_ge(S1[s]["hx_stored"], 16 * (IMAGES // 2) + 16)
            sp.wait_ge(S["weights_split"], 1)

            def hx_in(i):
                sp.wait_ge(S["hx_free"], i + 1)
                sp.dma_start(hx_row,
                             hx_store[:, bass.ds(i, 1), :].rearrange("p a n -> p (a n)")).then_inc(S["hx_back"], 16)

            def result_out(i):
                sp.wait_ge(S["out_ready"], i + 2)
                sp.dma_start(A["out"][:, bass.ds(i * NT, NT), :], res[:]).then_inc(S["out_sent"], 16)

            for i in range(3):
                hx_in(i)
            with sp.Fori(0, IMAGES - 3) as i:
                result_out(i)
                hx_in(i + 3)
            for i in range(IMAGES - 3, IMAGES):
                result_out(i)
            sp.wait_ge(S["out_sent"], 16 * IMAGES + 16)

        N_LOADS = 19

        @block.gpsimd
        def _(pool):
            setting = Steps(pool, S["pool_set"])
            settings = [(v1[:], 0.0), (mx[:], 0.0), (wt[:], 0.0), (gacc[:], 0.0),
                        (kx[64:96, :, :].bitcast(F32), 1.0), (wproj[:, 193:194], 0.0),
                        (v1[:, :, :, HD:HD + 1], 1.0)]
            for m in IM:
                settings += [(m.patch[D:D + 1, :], 1.0), (m.xt[D:D + 1, :], 1.0), (m.at[D:D + 1, :], 1.0),
                             (m.a1[:, :, D:], 1.0), (m.ke[:, :, D:], 1.0)]
            for ap, value in settings:
                setting.link(nc.gpsimd.memset(ap, value))
            pool.drain().then_inc(S["set_done"], 1)
            pool.wait_ge(S["loaded"], 16 * N_LOADS)
            half = con[0:TP, C_HALF:C_HALF + NT]

            def image(r, s):
                m, S = IM[s], S1[s]
                pool.wait_ge(S["var_ready"], r + 1)
                nc.gpsimd.tensor_tensor(m.st[:, 3, :], m.st[:, 2, :], half, ALU.pow).then_inc(S["rstd_ready"], 1)
                yield
                for layer, (given, out, done) in enumerate((("si1_ready", m.sp1, "slope1_ready"),
                                                            ("si2_ready", m.sp2, "slope2_ready"))):
                    yield
                    pool.wait_ge(S[given], r + 1)
                    nc.gpsimd.tensor_tensor(out, m.si, m.sg, ALU.mult).then_inc(S["pool_steps"], 1)
                    nc.gpsimd.tensor_tensor(m.sq, m.si, m.sg, ALU.add).then_inc(S["pool_steps"], 1)
                    pool.wait_ge(S["pool_steps"], 2 + 2 * layer + 4 * r)
                    nc.gpsimd.tensor_tensor(out, m.sq, out, ALU.subtract).then_inc(S[done], 1)
                    yield

            first_pass(pool, image)

            def rstd(stats, asked, given, count):
                pool.wait_ge(S[asked], count)
                nc.gpsimd.tensor_tensor(stats[:, 3, :], stats[:, 2, :], half, ALU.pow).then_inc(S[given], 1)
                pool.wait_ge(S[given], count)

            def before(i):
                for k in range(4):
                    yield
                rstd(st, "var_pre", "rstd_pre", 2 * i + 1)
                yield
                rstd(st, "var_pre", "rstd_pre", 2 * i + 2)
                pool.sem_inc(S["waited"], 1)
                nc.gpsimd.memset(qx[64:96, :, :].bitcast(F32), 0.0).then_inc(S["qx_zero"], 1)
                pool.wait_ge(S["qx_zero"], i + 1)
                yield

            def maxima(i):
                yield

            def scores(i):
                pool.wait_ge(S["xd_ready"], i + 1)
                pool.wait_ge(S["xd2_ready"], i + 1)
                pool.sem_inc(S["waited"], 1)
                nc.gpsimd.tensor_copy(h2_held[:], h2[:])
                nc.gpsimd.tensor_copy(x2_held[:], x2[:]).then_inc(S["held"], 1)
                pool.wait_ge(S["held"], i + 2)
                for kb in range(NT):
                    for hp in range(2):
                        pool.wait_ge(S["exp_done"], i * 22 + first_piece(kb) * 2 + hp + 1)
                        pool.sem_inc(S["waited"], 1)
                        d = pt[0:TP, kb % 2, 2 * hp:2 * hp + 2, kb * TP:(kb + 1) * TP]
                        nc.gpsimd.affine_select(out=d, in_=d, compare_op=ALU.is_ge, fill=0.0, base=0,
                                                pattern=[[0, 2], [1, TP]], channel_multiplier=-1
                                                ).then_inc(S["diag_done"], 1)

            def after(i):
                yield
                pool.wait_ge(S["rden_ready"], i + 1)
                pool.wait_ge(S["pv_saved"], 2 * i + 2)
                nc.gpsimd.tensor_tensor(yn[:], pv[:], rden[:], ALU.mult).then_inc(S["yn_ready"], 1)
                pool.wait_ge(S["yn_ready"], i + 1)
                yield
                rstd(st2, "var_post", "rstd_post", i + 1)
                yield

            def experts(j):
                for n in range(26):
                    if n % 3 == 1 and n > 1:
                        g = n // 3 - 1
                        c, p = g // PAIRS, g % PAIRS
                        w, cols = width(c), tok_cols(c)
                        pool.wait_ge(S["z_ready"], 8 * j + g + 1)
                        if p == 0:
                            pool.sem_inc(S["waited"], 1)
                            ins = nc.gpsimd.tensor_copy(zacc[:, cols], zz[:, g % 2, 0:w])
                        else:
                            ins = nc.gpsimd.tensor_tensor(zacc[:, cols], zacc[:, cols], zz[:, g % 2, 0:w], ALU.add)
                        ins.then_inc(S["z_added"], 1)
                        pool.wait_ge(S["z_added"], 8 * j + g + 1)
                    yield

            second_pass(pool, before, maxima, scores, after, experts)

        @block.tensor
        def _(pe):
            mm = nc.tensor.matmul

            def transposes(src, rows, b, ready):
                pe.sem_inc(S["waited"], 1)
                for c, (t0, t1) in enumerate(CHUNKS):
                    for t in range(t0, t1):
                        last = nc.tensor.transpose(P[0:rows, b + c, (t - t0) * TP:(t - t0 + 1) * TP],
                                                   src(t), ident[0:TP, 0:TP])
                    last.then_inc(ready, 1)

            pe.wait_ge(S["loaded"], 16 * N_LOADS)
            pe.wait_ge(S["set_done"], 1)
            mm(P[0:D, 0, 0:D], wk_t[:], ws[0:D, 0, :], start=True, stop=True).then_inc(S["wz0_ps"], 1)
            pe.wait_ge(S["wproj_ready"], 1)

            def tiled(b, lhs, rhs, ready):
                for t in range(NT):
                    last = mm(P[0:TP, b, t * D:(t + 1) * D], lhs(t), rhs, start=True, stop=True)
                last.then_inc(ready, 1)

            def image(r, s):
                m, S = IM[s], S1[s]
                b = m.bank
                tile = lambda t: slice(t * TP, (t + 1) * TP)
                pe.wait_ge(S["patch_in"], 16 * r + 16)
                pe.wait_ge(S["grads_summed"], r + 1)
                tiled(b, lambda t: m.patch[:, tile(t)], tokw[:], S["h_ps"])
                yield
                pe.wait_ge(S["x1_ready"], r + 1)
                transposes(lambda t: m.x1[:, t, :], D, b, S["xt_ps"])
                yield
                pe.wait_ge(S["xt_ready"], 6 * r + 2)
                for t in range(NT):
                    o = b * BANK + t * 256
                    last = mm(flat[0:TP, o:o + 194], m.xt[:, tile(t)], wproj[:], start=True, stop=True)
                last.then_inc(S["proj_ps"], 1)
                yield
                pe.wait_ge(S["values_read"], r + 1)
                transposes(lambda t: m.a1[:, t, 0:D], D, b, S["xt_ps"])
                yield
                pe.wait_ge(S["xt_ready"], 6 * r + 4)
                tiled(b + 2, lambda t: m.at[:, tile(t)], ws[:, 1, :], S["z2_ps"])
                yield
                pe.wait_ge(S["dz2_ready"], r + 1)
                transposes(lambda t: m.dz[:, t, :], D, b, S["xt_ps"])
                for t in range(NT):
                    mm(P[0:D + 1, b + 3, 256 + D:256 + 2 * D], m.a1[:, t, 0:D + 1], m.dz[:, t, :],
                       start=(t == 0), stop=(t == NT - 1))
                yield
                pe.wait_ge(S["xt_ready"], 6 * r + 6)
                tiled(b + 2, lambda t: m.xt[0:D, tile(t)], w1l_t[:], S["da_ps"])
                yield
                pe.wait_ge(S["dz1_ready"], r + 1)
                pe.wait_ge(S["keys_saved"], r + 1)
                for t in range(NT):
                    last = mm(P[0:D + 1, b + 3, 256:256 + D], m.ke[:, t, 0:D + 1], m.dz1[:, t, :],
                              start=(t == 0), stop=(t == NT - 1))
                last.then_inc(S["grad_ps"], 1)
                yield

            first_pass(pe, image)
            pe.wait_ge(S["nws_ready"], 1)
            mm(P[0:D, 0, 0:D], wq_t[:], nws[0:D, 0, :], start=True, stop=True).then_inc(S["wz_ps"], 1)
            pe.wait_ge(S["wqproj_ready"], 1)
            pe.wait_ge(S["weights_split"], 1)
            pe.sem_inc(S["hx_free"], 1)

            def turned(src):
                return lambda t: src[:, t, :, :].rearrange("p a f -> p (a f)")

            def before(i):
                pe.wait_ge(S["hx_back"], 16 * i + 16)
                transposes(lambda t: x1[:, t, :], D, 0, S["pre_ps"])
                yield
                pe.wait_ge(S["ar_ready"], 4 * i + 2)
                for t in range(NT):
                    last = mm(flat[0:TP, 2 * BANK + t * 128:2 * BANK + t * 128 + 128], xt[:, t * TP:(t + 1) * TP],
                              wqproj[:], start=True, stop=True)
                last.then_inc(S["pre_ps"], 1)
                yield
                pe.wait_ge(S["a1_used"], i + 1)
                transposes(lambda t: a1[:, t, 0:D], D, 0, S["pre_ps"])
                yield
                pe.wait_ge(S["ar_ready"], 4 * i + 4)
                for t in range(NT):
                    last = mm(P[0:TP, 2, t * D:(t + 1) * D], at[:, t * TP:(t + 1) * TP], nws[:, 1, :],
                              start=True, stop=True)
                last.then_inc(S["pre_ps"], 1)
                yield
                yield
                yield
                pe.wait_ge(S["xd_ready"], i + 1)
                transposes(turned(xd), 128, 0, S["xd_ps"])
                yield
                pe.wait_ge(S["xs_ready"], 2 * i + 2)
                for c in range(2):
                    for k in range(2):
                        for w in (wah, wal):
                            last = mm(P[0:QK, 2 - 2 * c + k, 0:width(c)], w[:, k * QK:(k + 1) * QK],
                                      xs[:, tok_cols(c)], start=(w is wah), stop=(w is wal))
                    last.then_inc(S["qk_ps"], 1)
                pe.wait_ge(S["rope_read"], 2 * i + 1)
                for t in range(NT):
                    for w in (wah, wal):
                        last = mm(P[0:TP, 2, t * 32:(t + 1) * 32], xs[:, t * TP:(t + 1) * TP], w[:, 2 * QK:],
                                  start=(w is wah), stop=(w is wal))
                last.then_inc(S["qk_ps"], 1)
                yield
                pe.wait_ge(S["qkl_ready"], i + 1)
                for o in range(3):
                    for c in range(2):
                        n = 2 * o + c
                        if o == 2:
                            pe.wait_ge(S["rows_act" if c == 0 else "rows_dve"], 3 * i + 1)
                        if n == 2:
                            pe.wait_ge(S["v_saved"], i + 1)
                        b = n % 4
                        mm(P[:, b, 0:width(c)], sel[0:QK, o, :], qkh[:, tok_cols(c)], start=True, stop=False)
                        mm(P[:, b, 0:width(c)], sel[0:QK, 3 + o, :], qkl[:, tok_cols(c)], start=False,
                           stop=True).then_inc(S["spread_ps"], 1)
                pe.wait_ge(S["rows_act"], 3 * i + 3)
                pe.wait_ge(S["rows_dve"], 3 * i + 3)
                yield

            def maxima(i):
                pe.wait_ge(S["qx_zero"], i + 1)
                for qt in range(NT):
                    for h in range(NH):
                        n = qt * NH + h
                        o = (n % 2) * BANK if qt < 4 else 0
                        if n >= 2:
                            pe.wait_ge(S["smax_read"], 28 * i + n - (1 if qt < 4 else 0))
                        keys = (qt + 1) * TP
                        for k0 in range(0, keys, BANK):
                            k1 = min(keys, k0 + BANK)
                            diag = max(k0, qt * TP)
                            mm(flat[0:TP, o + k0:o + k1], qx[:, h, qt * TP:keys], kx[:, h // 2, k0:k1],
                               start=True, stop=diag >= k1)
                            if diag < k1:
                                last = mm(flat[0:TP, o + diag:o + k1], idb[:],
                                          maskb[:, diag - qt * TP:k1 - qt * TP], start=False, stop=True)
                        last.then_inc(S["smax_ps"], 1)
                        yield

            def scores(i):
                pe.wait_ge(S["smax_read"], 28 * i + 28)
                for c, (t0, t1) in enumerate(CHUNKS):
                    for t in range(t0, t1):
                        last = mm(P[64:96, c, (t - t0) * TP:(t - t0 + 1) * TP], mx[:, t, :], ident[0:TP, 0:TP],
                                  start=True, stop=True)
                    last.then_inc(S["mxt_ps"], 1)
                pe.wait_ge(S["mrow_act"], 4 * i + 4)
                pe.wait_ge(S["mrow_dve"], 4 * i + 4)

                def weights(n):
                    kb, q0, q1 = PIECES[n]
                    for hp in range(2):
                        m = 2 * n + hp
                        if m >= 3:
                            pe.wait_ge(S["exp_done"], 22 * i + m - 2)
                        for j in range(2):
                            last = mm(P[0:TP, (m % 3) * 2 + j, 0:q1 - q0], kx[:, hp, kb * TP:(kb + 1) * TP],
                                      qx[:, 2 * hp + j, q0:q1], start=True, stop=True)
                        last.then_inc(S["st_ps"], 1)

                def values(n):
                    kb, q0, q1 = PIECES[n]
                    pe.wait_ge(S["exp_done"], 22 * i + 2 * n + 2)
                    if q0 == kb * TP:
                        pe.wait_ge(S["diag_done"], 14 * i + 2 * kb + 2)
                    c = q0 >= 448
                    for h in range(NH):
                        last = mm(P[32 * h:32 * h + 32, 6 + c, q0 - 448 * c:q1 - 448 * c], v1[:, kb, h // 2, :],
                                  pt[0:TP, kb % 2, h, q0:q1], start=(kb == 0), stop=(kb == (6 if c else 3)))
                    last.then_inc(S["pv_ps"], 1)

                weights(0)
                pe.wait_ge(S["out_ready"], i + 1)
                for n in range(1, len(PIECES) + 1):
                    if n < len(PIECES):
                        weights(n)
                    values(n - 1)

            def after(i):
                for c in range(2):
                    pe.wait_ge(S["pv_saved"], 2 * i + c + 1)
                    mm(P[:, 4 + c, 0:width(c)], con[:, C_DEN:C_DEN + 128], pv[:, tok_cols(c)], start=True,
                       stop=True).then_inc(S["den_ps"], 1)
                yield
                pe.wait_ge(S["yn_ready"], i + 1)
                for t in range(NT):
                    last = mm(P[0:TP, 6, t * D:(t + 1) * D], yn[:, t * TP:(t + 1) * TP], wo[:], start=True,
                              stop=True)
                last.then_inc(S["wo_ps"], 1)
                yield
                yield
                pe.wait_ge(S["xd2_ready"], i + 2)
                transposes(turned(xd2), 128, 4, S["xd2_ps"])
                yield
                pe.wait_ge(S["xm_ready"], 2 * i + 2)
                for t in range(NT):
                    for w in (wrh, wrl):
                        last = mm(P[0:TP, 7, t * NE:(t + 1) * NE], xm[:, t * TP:(t + 1) * TP], w[:],
                                  start=(w is wrh), stop=(w is wrl))
                last.then_inc(S["logit_ps"], 1)
                yield
                yield
                pe.wait_ge(S["wt_ready"], i + 1)
                transposes(lambda t: wt[:, t, :], 40, 4, S["wt_ps"])
                pe.wait_ge(S["wts_ready"], 2 * i + 2)
                yield

            def experts(j):
                def up(n):
                    c, p, k = n // 12, n // 3 % 4, n % 3
                    m = TAIL_W if k == 2 else MAIN
                    for b, ready, freed in ((2, "h1_ps", "silu_done"), (4, "h3_ps", "hh_ready")):
                        if n >= 2:
                            pe.wait_ge(S[freed], 24 * j + n - 1)
                        o = p * PAIR_W + k * MAIN + (b // 4) * PAIRS * PAIR_W
                        for w in (wmh, wml):
                            last = mm(P[0:m, b + n % 2, 0:width(c)], w[:, o:o + m], xm[:, tok_cols(c)],
                                      start=(w is wmh), stop=(w is wml))
                        last.then_inc(S[ready], 1)

                def down(g):
                    c, p = g // 4, g % 4
                    w = width(c)
                    if g >= 1:
                        pe.wait_ge(S["bw_saved"], 8 * j + g)
                    mm(P[:, 7, 0:w], selp[:, p, :], wts[:, tok_cols(c)], start=True,
                       stop=True).then_inc(S["bw_ps"], 1)
                    pe.wait_ge(S["hh_ready"], 24 * j + 3 * g + 3)
                    if g >= 1:
                        pe.wait_ge(S["z_ready"], 8 * j + g)
                    for e in range(2):
                        mm(P[64 * e:64 * e + 64, 6, 0:w], w2[:, 3 * p + e, :], hh[:, g % 2, e, 0:w], start=True,
                           stop=False)
                    for e in range(2):
                        last = mm(P[64 * e:64 * e + 64, 6, 0:w], w2[64 * e:64 * e + TAIL, 3 * p + 2, :],
                                  hh[64 * e:64 * e + TAIL, g % 2, 2, 0:w], start=False, stop=True)
                    last.then_inc(S["y_ps"], 1)

                for n in range(25):
                    if n < 24:
                        up(n)
                    if n % 3 == 0 and n:
                        down(n // 3 - 1)
                    yield
                pe.wait_ge(S["z_added"], 8 * j + 8)
                for t in range(NT):
                    last = mm(P[0:TP, 6, t * D:(t + 1) * D], zacc[:, t * TP:(t + 1) * TP],
                              con[:, C_FOLD:C_FOLD + 64], start=True, stop=True)
                last.then_inc(S["fold_ps"], 1)
                yield

            second_pass(pe, before, maxima, scores, after, experts)

        @block.scalar
        def _(act):
            copy = lambda out, in_: nc.scalar.activation(out, in_, ACT.Copy)

            def evacuate(dst, rows, b, ps, ready, i, per, n):
                for c in range(2):
                    act.wait_ge(S[ps], i * per + n + c)
                    copy(dst[0:rows, tok_cols(c)], P[0:rows, b + c, 0:width(c)]).then_inc(S[ready], 1)

            act.wait_ge(S["set_done"], 1)

            def image(r, s):
                m, S = IM[s], S1[s]
                b = m.bank

                def evacuate(dst, n):
                    for c in range(2):
                        act.wait_ge(S["xt_ps"], 6 * r + n + c)
                        copy(dst[0:D, tok_cols(c)], P[0:D, b + c, 0:width(c)]).then_inc(S["xt_ready"], 1)

                act.wait_ge(S["h_ps"], r + 1)
                act.wait_ge(S["hx_stored"], 16 * r + 16)
                copy(m.h, tiles(b)).then_inc(S["h_saved"], 1)
                yield
                evacuate(m.xt, 1)
                yield
                act.wait_ge(S["proj_ps"], r + 1)
                pr = flat[0:TP, b * BANK:b * BANK + NT * 256].rearrange("p (t f) -> p t f", f=256)
                nc.scalar.activation(m.sg, pr[:, :, 0:D], ACT.Sigmoid).then_inc(S["sig1"], 1)
                copy(m.ke[:, :, 0:D], pr[:, :, D:2 * D]).then_inc(S["keys_saved"], 1)
                nc.scalar.activation(m.st[:, 4, :], pr[:, :, 192], ACT.Sigmoid).then_inc(S["alr_ready"], 1)
                yield
                evacuate(m.at, 3)
                yield
                act.wait_ge(S["z2_ps"], r + 1)
                act.wait_ge(S["slope1_ready"], r + 1)
                nc.scalar.activation(m.sg, tiles(b + 2), ACT.Sigmoid).then_inc(S["sig2"], 1)
                yield
                evacuate(m.xt, 5)
                yield

            first_pass(act, image)

            def before(i):
                evacuate(xt, D, 0, "pre_ps", "ar_ready", i, 6, 1)
                yield
                act.wait_ge(S["pre_ps"], 6 * i + 3)
                zq = flat[0:TP, 2 * BANK:2 * BANK + NT * 128].rearrange("p (t f) -> p t f", f=128)
                nc.scalar.activation(sg[:], zq[:, :, 0:D], ACT.Tanh, scale=0.5).then_inc(S["tanh_z"], 1)
                yield
                evacuate(at, D, 0, "pre_ps", "ar_ready", i, 6, 4)
                yield
                act.wait_ge(S["pre_ps"], 6 * i + 6)
                nc.scalar.activation(sg[:], tiles(2), ACT.Tanh, scale=0.5).then_inc(S["tanh_z2"], 1)
                yield
                yield
                yield
                evacuate(xh, 128, 0, "xd_ps", "xh_ready", i, 2, 1)
                yield
                act.wait_ge(S["qk_ps"], 3 * i + 3)
                v = P[0:TP, 2, 0:NT * 32].rearrange("p (t g d) -> p t g d", g=NKV, d=HD)
                for g in range(NKV):
                    last = copy(v1[:, :, g, 0:HD], v[:, :, g, :])
                last.then_inc(S["v_saved"], 1)
                act.wait_ge(S["rope_done"], i + 1)
                copy(qkh[:], qk[:]).then_inc(S["qkh_ready"], 1)
                yield
                for o in range(3):
                    act.wait_ge(S["spread_ps"], 6 * i + 2 * o + 1)
                    spread_rows(copy, o, 0).then_inc(S["rows_act"], 1)
                yield

            def maxima(i):
                yield

            def scores(i):
                act.wait_ge(S["mxt_ps"], 2 * i + 1)
                for h in range(NH):
                    nc.scalar.activation(qx[64:96, h, tok_cols(0)], P[64:96, 0, 0:width(0)], ACT.Copy,
                                         scale=con[64:96, C_MAXROW + h:C_MAXROW + h + 1]
                                         ).then_inc(S["mrow_act"], 1)
                for n, (kb, q0, q1) in enumerate(PIECES):
                    if kb >= 2:
                        act.wait_ge(S["pv_ps"], 11 * i + first_piece(kb - 1))
                    for hp in range(2):
                        m = 2 * n + hp
                        act.wait_ge(S["st_ps"], 22 * i + m + 1)
                        b = (m % 3) * 2
                        nc.scalar.activation(pt[0:TP, kb % 2, 2 * hp:2 * hp + 2, q0:q1],
                                             P[0:TP, b:b + 2, 0:q1 - q0], ACT.Exp,
                                             scale=float(HD) ** -0.5).then_inc(S["exp_done"], 1)

            def after(i):
                act.wait_ge(S["pv_ps"], 11 * i + 11)
                for c in range(2):
                    copy(pv[:, tok_cols(c)], P[:, 6 + c, 0:width(c)]).then_inc(S["pv_saved"], 1)
                yield
                yield
                yield
                evacuate(xmh, 128, 4, "xd2_ps", "xmh_ready", i, 2, 1)
                yield
                act.wait_ge(S["logit_read"], i + 1)
                nc.scalar.activation(rt[:, 1, :, :], rt[:, 0, :, :], ACT.Exp).then_inc(S["exp_r"], 1)
                yield
                yield
                evacuate(wth, 40, 4, "wt_ps", "wth_ready", i, 2, 1)
                yield

            def experts(j):
                for n in range(25):
                    if n < 24:
                        w = width(n // 12)
                        r = TAIL_W if n % 3 == 2 else MAIN
                        act.wait_ge(S["h1_ps"], 24 * j + n + 1)
                        if n >= 2:
                            act.wait_ge(S["hh_ready"], 24 * j + n - 1)
                        nc.scalar.activation(su[0:r, n % 2, 0:w], P[0:r, 2 + n % 2, 0:w],
                                             ACT.Silu).then_inc(S["silu_done"], 1)
                    if n % 3 == 0 and n:
                        g = n // 3 - 1
                        w = width(g // 4)
                        act.wait_ge(S["bw_ps"], 8 * j + g + 1)
                        if g >= 2:
                            act.wait_ge(S["z_ready"], 8 * j + g - 1)
                        copy(bw[:, g % 2, 0:w], P[:, 7, 0:w]).then_inc(S["bw_saved"], 1)
                    yield

            second_pass(act, before, maxima, scores, after, experts)

        @block.vector
        def _(dve):
            V = nc.vector
            chain = Steps(dve, S["dve_steps"])
            link = chain.link

            def over_tiles(s, n=D):
                return s.unsqueeze(2).broadcast_to([TP, NT, n])

            def mean_rstd(src, centre, var, rstd, n, link, st=st, sq=sq[:], xc=xc[:]):
                if centre:
                    link(V.reduce_sum(st[:, 0, :], src, axis=AX.X))
                    link(V.tensor_scalar(st[:, 1, :], st[:, 0, :], 1.0 / D, None, ALU.mult))
                    link(V.tensor_tensor(xc, src, over_tiles(st[:, 1, :]), ALU.subtract))
                    src = xc
                link(V.tensor_tensor(sq, src, src, ALU.mult))
                link(V.reduce_sum(st[:, 5, :], sq, axis=AX.X))
                V.tensor_scalar(st[:, 2, :], st[:, 5, :], 1.0 / D, EPS_LN if centre else EPS_RMS, ALU.mult,
                                ALU.add).then_inc(var, 1)
                dve.wait_ge(rstd, n)

            dve.wait_ge(S["loaded"], 16 * N_LOADS)
            dve.wait_ge(S["set_done"], 1)
            V.tensor_copy(sel[:], con[:, C_SELH:C_SELH + 768].rearrange("p (o r) -> p o r", o=6))
            V.tensor_copy(selp[:], con[0:40, C_PAIR:C_PAIR + PAIRS * 128].rearrange("p (o r) -> p o r", o=PAIRS))
            V.tensor_copy(idb[:], con[0:TP, C_ID:C_ID + TP])
            V.tensor_copy(maskb[:], con[0:TP, C_MASK:C_MASK + TP])
            for raw, hi, lo, ln in ((araw, wah, wal, 0), (rraw, wrh, wrl, 1), (mraw, wmh, wml, 1)):
                link(V.tensor_scalar(raw[:], raw[:], lnw[:, ln:ln + 1], None, ALU.mult))
                link(V.tensor_copy(hi[:], raw[:]))
                last = V.tensor_tensor(lo[:], raw[:], hi[:].bitcast(F32), ALU.subtract)
            last.then_inc(S["weights_split"], 1)
            dve.wait_ge(S["wz0_ps"], 1)
            V.tensor_copy(wproj[0:D, 0:D], P[0:D, 0, 0:D])
            V.tensor_copy(wproj[D:D + 1, 0:D], ws[D:D + 1, 0, :]).then_inc(S["wproj_ready"], 1)
            for s in range(2):
                dve.sem_inc(S1[s]["patch_used"], 1)
                dve.sem_inc(S1[s]["hx_stored"], 16)
                dve.sem_inc(S1[s]["grads_summed"], 1)
            dve.sem_inc(S["out_sent"], 16)
            dve.sem_inc(S["out_ready"], 1)
            dve.sem_inc(S["held"], 1)
            dve.sem_inc(S["xd2_ready"], 1)
            chains = [Steps(dve, S1[s]["dve_steps"]) for s in range(2)]

            def image(r, s):
                m, S = IM[s], S1[s]
                chains[s].round(r, D1)
                link, b = chains[s].link, m.bank
                dve.wait_ge(S["h_saved"], r + 1)
                dve.sem_inc(S["patch_used"], 1)
                mean_rstd(m.h, True, S["var_ready"], S["rstd_ready"], r + 1, link, m.st, m.sq, m.xc)
                V.tensor_tensor(m.x1, m.xc, over_tiles(m.st[:, 3, :]), ALU.mult).then_inc(S["x1_ready"], 1)
                yield
                yield
                pr = flat[0:TP, b * BANK:b * BANK + NT * 256].rearrange("p (t f) -> p t f", f=256)
                dve.wait_ge(S["alr_ready"], r + 1)
                V.tensor_tensor(m.si, pr[:, :, 0:D], m.sg, ALU.mult).then_inc(S["si1_ready"], 1)
                dve.wait_ge(S["si1_ready"], r + 1)
                V.tensor_tensor(m.a1[:, :, 0:D], m.ke[:, :, 0:D], m.si, ALU.add).then_inc(S["a1_ready"], 1)
                dve.wait_ge(S["a1_ready"], r + 1)
                V.tensor_tensor(m.xc, m.a1[:, :, 0:D], pr[:, :, 2 * D:3 * D],
                                ALU.subtract).then_inc(S["values_read"], 1)
                link(V.tensor_scalar(m.st[:, 6, :], m.st[:, 4, :], MAX_ALR * 2.0 / D, None, ALU.mult))
                yield
                yield
                dve.wait_ge(S["sig2"], r + 1)
                V.tensor_tensor(m.si, tiles(b + 2), m.sg, ALU.mult).then_inc(S["si2_ready"], 1)
                dve.wait_ge(S["si2_ready"], r + 1)
                link(V.tensor_tensor(m.xc, m.xc, m.si, ALU.add))
                link(V.tensor_tensor(m.dp, m.xc, over_tiles(m.st[:, 6, :]), ALU.mult))
                dve.wait_ge(S["slope2_ready"], r + 1)
                V.tensor_tensor(m.dz, m.dp, m.sp2, ALU.mult).then_inc(S["dz2_ready"], 1)
                yield
                yield
                dve.wait_ge(S["da_ps"], r + 1)
                link(V.tensor_tensor(m.xc, tiles(b + 2), m.dp, ALU.add))
                V.tensor_tensor(m.dz1, m.xc, m.sp1, ALU.mult).then_inc(S["dz1_ready"], 1)
                yield
                dve.wait_ge(S["grad_ps"], r + 1)
                V.tensor_tensor(gacc[:], gacc[:], P[0:D + 1, b + 3, 256:256 + 2 * D].rearrange(
                    "p (l n) -> p l n", l=2), ALU.add).then_inc(S["grads_summed"], 1)
                dve.wait_ge(S["grads_summed"], r + 2)
                assert chains[s].n == D1, chains[s].n
                yield

            first_pass(dve, image)
            link(V.tensor_scalar(gtmp[:], gacc[:], -1.0, None, ALU.mult))
            link(V.tensor_tensor(gtmp[:], gacc[:], gtmp[:], ALU.max))
            link(V.tensor_scalar(gtmp[:], gtmp[:], EPS_ADAM, None, ALU.add))
            link(V.reciprocal(gtmp[:], gtmp[:]))
            link(V.tensor_tensor(gtmp[:], gacc[:], gtmp[:], ALU.mult))
            link(V.tensor_scalar(gtmp[:], gtmp[:], LR, None, ALU.mult))
            link(V.tensor_scalar(nws[:], ws[:], 1.0 - LR * WD, None, ALU.mult))
            V.tensor_tensor(nws[:], nws[:], gtmp[:], ALU.subtract).then_inc(S["nws_ready"], 1)
            dve.wait_ge(S["nws_ready"], 1)
            dve.wait_ge(S["wz_ps"], 1)
            V.tensor_copy(wqproj[0:D, 0:D], P[0:D, 0, 0:D])
            V.tensor_copy(wqproj[D:D + 1, 0:D], nws[D:D + 1, 0, :]).then_inc(S["wqproj_ready"], 1)
            rs = lambda k: rt[:, k, :, :]

            def normed(src, i, link, stats, squares, var, rstd, count, dup, ready):
                mean_rstd(src, False, S[var], S[rstd], count, link, stats, squares)
                V.tensor_tensor(dup[:], src.unsqueeze(2).broadcast_to([TP, NT, 2, D]),
                                stats[:, 3, :].unsqueeze(2).unsqueeze(3).broadcast_to([TP, NT, 2, D]),
                                ALU.mult).then_inc(S[ready], 1)

            def low_parts(dst, high, low, b, given, ready, i):
                r = dst.shape[0]
                for c in range(2):
                    dve.wait_ge(S[given], 2 * i + c + 1)
                    V.scalar_tensor_tensor(dst[:, tok_cols(c)], high[:, tok_cols(c)].bitcast(F32),
                                           con[0:r, low:low + 1], P[0:r, b + c, 0:width(c)], ALU.mult,
                                           ALU.add).then_inc(S[ready], 1)

            pre = Steps(dve, S["pre_steps"])
            post = Steps(dve, S["post_steps"])

            def before(i):
                pre.round(i, D_PRE)
                yield
                yield
                zq = flat[0:TP, 2 * BANK:2 * BANK + NT * 128].rearrange("p (t f) -> p t f", f=128)
                dve.wait_ge(S["tanh_z"], i + 1)
                pre.link(V.scalar_tensor_tensor(sq[:], sg[:], 1.0, zq[:, :, 0:D], ALU.add, ALU.mult))
                V.scalar_tensor_tensor(a1[:, :, 0:D], sq[:], 0.5, zq[:, :, D:], ALU.mult,
                                       ALU.add).then_inc(S["a1_used"], 1)
                dve.wait_ge(S["held"], i + 1)
                dve.wait_ge(S["a1_used"], i + 1)
                pre.link(V.tensor_tensor(h2[:], a1[:, :, 0:D], h_in, ALU.add))
                dve.sem_inc(S["hx_free"], 1)
                yield
                dve.wait_ge(S["tanh_z2"], i + 1)
                pre.link(V.scalar_tensor_tensor(sq[:], sg[:], 1.0, tiles(2), ALU.add, ALU.mult))
                pre.link(V.scalar_tensor_tensor(h2[:], sq[:], 0.5, h2[:], ALU.mult, ALU.add))
                yield
                mean_rstd(h2[:], True, S["var_pre"], S["rstd_pre"], 2 * i + 1, pre.link)
                yield
                pre.link(V.tensor_tensor(x2[:], xc[:], over_tiles(st[:, 3, :]), ALU.mult))
                normed(x2[:], i, pre.link, st, sq[:], "var_pre", "rstd_pre", 2 * i + 2, xd, "xd_ready")
                yield
                low_parts(xs, xh, C_LOW64, 0, "xh_ready", "xs_ready", i)
                yield
                for c in range(2):
                    dve.wait_ge(S["qk_ps"], 3 * i + c + 1)
                    b = 2 - 2 * c
                    V.tensor_tensor(qk[:, tok_cols(c)], P[0:QK, b, 0:width(c)], rope[:, 0, tok_cols(c)], ALU.mult)
                    V.tensor_tensor(qk_sin[:, tok_cols(c)], P[0:QK, b + 1, 0:width(c)], rope[:, 1, tok_cols(c)],
                                    ALU.mult).then_inc(S["rope_read"], 1)
                dve.wait_ge(S["rope_read"], 2 * i + 2)
                V.tensor_tensor(qk[:], qk[:], qk_sin[:], ALU.add).then_inc(S["rope_done"], 1)
                dve.wait_ge(S["qkh_ready"], i + 1)
                V.tensor_tensor(qkl[:], qk[:], qkh[:].bitcast(F32), ALU.subtract).then_inc(S["qkl_ready"], 1)
                yield
                for o in range(3):
                    dve.wait_ge(S["spread_ps"], 6 * i + 2 * o + 2)
                    spread_rows(V.tensor_copy, o, 1).then_inc(S["rows_dve"], 1)
                assert pre.n == D_PRE, pre.n
                yield

            def maxima(i):
                for qt in range(NT):
                    for h in range(NH):
                        n = qt * NH + h
                        dve.wait_ge(S["smax_ps"], 28 * i + n + 1)
                        o = (n % 2) * BANK if qt < 4 else 0
                        V.reduce_max(mx[:, qt, h:h + 1], flat[0:TP, o:o + (qt + 1) * TP],
                                     axis=AX.X).then_inc(S["smax_read"], 1)
                        yield

            def scores(i):
                dve.wait_ge(S["mxt_ps"], 2 * i + 2)
                for h in range(NH):
                    V.tensor_scalar(qx[64:96, h, tok_cols(1)], P[64:96, 1, 0:width(1)],
                                    con[64:96, C_MAXROW + h:C_MAXROW + h + 1], None,
                                    ALU.mult).then_inc(S["mrow_dve"], 1)

            rank = con[0:TP, C_RANK:C_RANK + NT * NE].rearrange("p (t e) -> p t e", e=NE)

            def after(i):
                post.round(i, D_POST)
                link = post.link
                for c in range(2):
                    dve.wait_ge(S["den_ps"], 2 * i + c + 1)
                    ins = V.reciprocal(rden[:, tok_cols(c)], P[:, 4 + c, 0:width(c)])
                ins.then_inc(S["rden_ready"], 1)
                yield
                dve.wait_ge(S["wo_ps"], i + 1)
                link(V.tensor_tensor(x2_held[:], x2_held[:], tiles(6), ALU.add))
                V.tensor_tensor(rest[:], h2_held[:], x2_held[:], ALU.add).then_inc(S["rest_ready"], 1)
                yield
                normed(x2_held[:], i, link, st2, sq2[:], "var_post", "rstd_post", i + 1, xd2, "xd2_ready")
                yield
                low_parts(xm, xmh, C_LOW64, 4, "xmh_ready", "xm_ready", i)
                yield
                dve.wait_ge(S["logit_ps"], i + 1)
                lg = P[0:TP, 7, 0:NT * NE].rearrange("p (t e) -> p t e", e=NE)
                link(V.reduce_max(st2[:, 0, :], lg, axis=AX.X))
                V.tensor_tensor(rs(0), lg, over_tiles(st2[:, 0, :], NE), ALU.subtract).then_inc(S["logit_read"], 1)
                yield
                dve.wait_ge(S["exp_r"], i + 1)
                link(V.reduce_sum(st2[:, 1, :], rs(1), axis=AX.X))
                link(V.reciprocal(st2[:, 1, :], st2[:, 1, :]))
                link(V.tensor_tensor(rs(1), rs(1), over_tiles(st2[:, 1, :], NE), ALU.mult))
                src = rs(1)
                for k in range(2):
                    link(V.reduce_max(st2[:, 4 + k, :], src, axis=AX.X))
                    link(V.tensor_tensor(rs(3), src, over_tiles(st2[:, 4 + k, :], NE), ALU.is_equal))
                    link(V.tensor_tensor(rs(3), rs(3), rank, ALU.mult))
                    link(V.reduce_max(st2[:, 6, :], rs(3), axis=AX.X))
                    link(V.tensor_tensor(rs(4 + k), rank, over_tiles(st2[:, 6, :], NE), ALU.is_equal))
                    if k == 0:
                        link(V.scalar_tensor_tensor(rs(2), rs(4), -2.0, rs(1), ALU.mult, ALU.add))
                        src = rs(2)
                link(V.tensor_tensor(rs(5), rs(5), rs(4), ALU.add))
                link(V.tensor_tensor(rs(1), rs(1), rs(5), ALU.mult))
                link(V.reduce_sum(st2[:, 6, :], rs(1), axis=AX.X))
                link(V.tensor_scalar(st2[:, 6, :], st2[:, 6, :], EPS_TOP, None, ALU.add))
                link(V.reciprocal(st2[:, 6, :], st2[:, 6, :]))
                link(V.tensor_tensor(wt[:, :, 0:NE], rs(1), over_tiles(st2[:, 6, :], NE), ALU.mult))
                V.tensor_copy(wt[:, :, 32:40], wt[:, :, 0:NE]).then_inc(S["wt_ready"], 1)
                yield
                low_parts(wts, wth, C_LOW32, 4, "wth_ready", "wts_ready", i)
                assert post.n == D_POST, post.n
                yield

            def experts(j):
                for n in range(26):
                    if n < 24:
                        w = width(n // 12)
                        r = TAIL_W if n % 3 == 2 else MAIN
                        g = n // 3
                        dve.wait_ge(S["silu_done"], 24 * j + n + 1)
                        dve.wait_ge(S["h3_ps"], 24 * j + n + 1)
                        if g >= 2:
                            dve.wait_ge(S["y_ps"], 8 * j + g - 1)
                        V.tensor_tensor(hh[0:r, g % 2, n % 3, 0:w], su[0:r, n % 2, 0:w],
                                        P[0:r, 4 + n % 2, 0:w], ALU.mult).then_inc(S["hh_ready"], 1)
                    if n % 3 == 1 and n > 1:
                        g = n // 3 - 1
                        w = width(g // 4)
                        dve.wait_ge(S["y_ps"], 8 * j + g + 1)
                        dve.wait_ge(S["bw_saved"], 8 * j + g + 1)
                        if g >= 2:
                            dve.wait_ge(S["z_added"], 8 * j + g - 1)
                        V.tensor_tensor(zz[:, g % 2, 0:w], bw[:, g % 2, 0:w], P[:, 6, 0:w],
                                        ALU.mult).then_inc(S["z_ready"], 1)
                    yield
                dve.wait_ge(S["fold_ps"], j + 1)
                dve.wait_ge(S["out_sent"], j * 16 + 16)
                V.tensor_tensor(res[:], rest[:], tiles(6), ALU.add).then_inc(S["out_ready"], 1)
                yield

            second_pass(dve, before, maxima, scores, after, experts)


PIECES = [(kb, q0, q1) for kb in range(NT)
          for q0, q1 in (((kb * TP, 448), (448, TOK)) if kb < 4 else ((kb * TP, TOK),))]


def first_piece(kb):
    return next(n for n, p in enumerate(PIECES) if p[0] == kb)


def lay_out(x, L0_tok_W, L0_tok_b, L0_attn_Wk, L0_attn_Wq, L0_attn_Wv, L0_attn_Wlr, L0_attn_blr, L0_attn_Ws,
            L0_attn_bs, L0_ffn_ln1_w, L0_ffn_ln2_w, L0_ffn_wq, L0_ffn_wk, L0_ffn_wv, L0_ffn_wo, L0_ffn_router_w,
            L0_ffn_w1, L0_ffn_w2, L0_ffn_w3):
    n = SIDE
    patches = x.reshape(IMAGES, n, PATCH, n, PATCH).transpose(2, 4, 0, 1, 3).reshape(D, IMAGES * TOK)
    col = lambda a: a.reshape(1, -1)
    zero = lambda *s: np.zeros(s, np.float32)
    wproj = np.concatenate([
        np.concatenate([L0_attn_Wk, L0_attn_Wv, L0_attn_Wlr], 1),
        np.concatenate([zero(1, 2 * D), col(L0_attn_blr)], 1)], 0)
    half = HD // 2
    swap = (np.arange(QK) // HD) * HD + (np.arange(QK) % HD + half) % HD
    wqk = np.concatenate([L0_ffn_wq, L0_ffn_wk], 0)
    attnw = np.concatenate([wqk, wqk[swap], L0_ffn_wv], 0).T
    pairs = []
    for w in (L0_ffn_w1, L0_ffn_w3):
        for p in range(PAIRS):
            e, f = w[2 * p], w[2 * p + 1]
            pairs += [e[:MAIN], f[:MAIN], e[MAIN:], zero(64 - TAIL, D), f[MAIN:]]
    w13 = np.concatenate(pairs, 0).T
    w2 = zero(128, 3 * PAIRS, D)
    for p in range(PAIRS):
        for k in range(2):
            t = L0_ffn_w2[2 * p + k].T
            w2[:, 3 * p + k] = t[:MAIN]
            w2[64 * k:64 * k + TAIL, 3 * p + 2] = t[MAIN:]
    wo = zero(128, D)
    for h in range(NH):
        wo[32 * h:32 * h + HD] = L0_ffn_wo[:, h * HD:(h + 1) * HD].T
    con, rope = shape_constants()
    out = {
        "con": con, "rope": rope, "patches": patches,
        "tokw": np.concatenate([L0_tok_W.T, col(L0_tok_b)], 0),
        "wk_t": L0_attn_Wk.T, "wq_t": L0_attn_Wq.T, "w1l_t": L0_attn_Ws[1].T,
        "ws": np.concatenate([L0_attn_Ws.transpose(1, 0, 2), L0_attn_bs[None]], 0),
        "wproj": wproj, "wqp": np.concatenate([L0_attn_Wq, zero(1, D)], 0),
        "attnw": attnw, "router": L0_ffn_router_w.T, "lnw": np.stack([L0_ffn_ln1_w, L0_ffn_ln2_w], 1),
        "w13": w13, "w2": w2, "wo": wo,
    }
    return {k: np.ascontiguousarray(v) for k, v in out.items()}


def kernel(**inputs):
    import concourse.bacc as bacc
    from concourse.bass_utils import run_bass_kernel_spmd

    arrays = lay_out(**{k: np.asarray(v) for k, v in inputs.items()})
    nc = bacc.Bacc("TRN2", target_bir_lowering=False, num_devices=1)
    aps = {k: nc.dram_tensor(f"in_{k}", v.shape, F32, kind="ExternalInput").ap() for k, v in arrays.items()}
    out = nc.dram_tensor("out_tokens", (IMAGES * TOK, D), F32, kind="ExternalOutput").ap()
    aps["out"] = out.rearrange("(t p) f -> p t f", p=TP)
    vit_block(nc, aps)
    r = run_bass_kernel_spmd(nc, [{f"in_{k}": v for k, v in arrays.items()}], core_ids=[0])
    return r.results[0]["out_tokens"].reshape(IMAGES, TOK, D)
```

```python
from contextlib import ExitStack

import numpy as np

import concourse.bass as bass
from concourse import mybir

F32 = mybir.dt.float32
F32R = mybir.dt.float32r
BF16 = mybir.dt.bfloat16
ALU = mybir.AluOpType
ACT = mybir.ActivationFunctionType
AX = mybir.AxisListType

IMAGES = 16
SIDE = 28
TOK = SIDE * SIDE
TP = 112
NT = TOK // TP
D = 64
PATCH = 8
NH, NKV, HD = 4, 2, 16
QK = (NH + NKV) * HD
NE, HID = 8, 170
PAIRS = NE // 2
MAIN = 128
TAIL = HID - MAIN
TAIL_W = 64 + TAIL
PAIR_W = 2 * MAIN + TAIL_W
CHUNKS = [(0, 4), (4, 7)]
BANK = 512
FILLS = sum(-(-(qt + 1) * TP // BANK) for qt in range(NT)) * NH
LR, WD, MAX_ALR, EPS_ADAM = 0.001, 0.01, 0.1, 1e-8
EPS_LN, EPS_RMS, EPS_TOP = 1e-5, 1e-6, 1e-9
NEG = -1e30
Q_ROWS = 96

C_ID = 0
C_MASK = C_ID + 128
C_SELH = C_MASK + TP
C_SELL = C_SELH + 3 * 128
C_PAIR = C_SELL + 3 * 128
C_DEN = C_PAIR + PAIRS * 128
C_FOLD = C_DEN + 128
C_LOW64 = C_FOLD + 64
C_LOW32 = C_LOW64 + 1
C_MAXROW = C_LOW32 + 1
C_RANK = C_MAXROW + NH
C_HALF = C_RANK + NT * NE
C_ALL = C_HALF + NT


def shape_constants():
    c = np.zeros((128, C_ALL), np.float32)
    c[:, C_ID:C_ID + 128] = np.eye(128)
    c[:TP, C_MASK:C_MASK + TP] = np.triu(np.full((TP, TP), NEG), 1)
    for out in range(3):
        for r in range(128):
            part, d = (r % 64) // 16, r % 16
            src = (out * 2 + r // 64) * HD + d
            low = part % 2 if out < 2 else part // 2
            c[src, (C_SELL if low else C_SELH) + out * 128 + r] = 1
    for p in range(PAIRS):
        for r in range(128):
            e = 2 * p + r // 64
            c[e, C_PAIR + p * 128 + r] = 1
            c[32 + e, C_PAIR + p * 128 + r] = 1
    for r in range(128):
        c[32 * (r // 32) + HD, C_DEN + r // 32] = 1
    c[:, C_FOLD:C_FOLD + 64] = np.concatenate([np.eye(64), np.eye(64)])
    c[64:, C_LOW64] = -1
    c[32:64, C_LOW32] = -1
    for h in range(NH):
        c[64 + h, C_MAXROW + h] = -1
    c[:, C_RANK:C_RANK + NT * NE] = np.tile(np.arange(NE, 0, -1), NT)
    c[:, C_HALF:C_HALF + NT] = -0.5
    inv = 1.0 / 10000.0 ** (np.arange(0, HD, 2, dtype=np.float32) / HD)
    freqs = np.outer(np.arange(TOK, dtype=np.float32), inv)
    emb = np.concatenate([freqs, freqs], -1)
    sign = np.where(np.arange(HD) < HD // 2, -1, 1).astype(np.float32)
    cos = np.tile(np.cos(emb).T, (NH + NKV, 1))
    sin = np.tile((np.sin(emb) * sign).T, (NH + NKV, 1))
    return c, np.stack([cos, sin], 1).astype(np.float32)


class Image:

    def __init__(self, patch, hx_row, h, x1, xt, at, a1, ke, xc, sq, sg, si, sp1, sp2, dp, dz, dz1, st, bank):
        self.patch, self.hx_row, self.h, self.x1, self.xt, self.at = patch, hx_row, h, x1, xt, at
        self.a1, self.ke, self.xc, self.sq, self.sg, self.si = a1, ke, xc, sq, sg, si
        self.sp1, self.sp2, self.dp, self.dz, self.dz1, self.st = sp1, sp2, dp, dz, dz1, st
        self.bank = bank


class Steps:

    def __init__(self, eng, sem):
        self.eng, self.sem, self.start, self.n, self.base = eng, sem, 0, 0, 0

    def round(self, i, per, done=0):
        self.n, self.base = done, self.start + i * per

    def link(self, ins):
        self.n += 1
        ins.then_inc(self.sem, 1)
        self.eng.wait_ge(self.sem, self.base + self.n)


def vit_block(nc, A):
    ctx = ExitStack()
    with ctx:
        def sb(name, shape, dt=F32):
            return ctx.enter_context(nc.sbuf_tensor(name, shape, dt))

        def sem(name):
            return ctx.enter_context(nc.semaphore(name))

        con = sb("con", [128, C_ALL])
        rope = sb("rope", [QK, 2, TOK])
        sel = sb("sel", [128, 6, 128], F32R)
        selp = sb("selp", [40, PAIRS, 128], F32R)
        idb = sb("idb", [TP, TP], BF16)
        maskb = sb("maskb", [TP, TP], BF16)
        ident = con[:, C_ID:C_ID + 128]
        tokw = sb("tokw", [D + 1, D])
        wk_t = sb("wk_t", [D, D])
        wq_t = sb("wq_t", [D, D])
        w1l_t = sb("w1l_t", [D, D])
        ws = sb("ws", [D + 1, 2, D])
        nws = sb("nws", [D + 1, 2, D])
        wproj = sb("wproj", [D + 1, 194])
        wqproj = sb("wqproj", [D + 1, 2 * D])
        NA = 2 * QK + NKV * HD
        NB = NE
        araw = sb("araw", [128, NA])
        wah = sb("wah", [128, NA], F32R)
        wal = sb("wal", [128, NA], F32R)
        rraw = sb("rraw", [128, NB])
        wrh = sb("wrh", [128, NB], F32R)
        wrl = sb("wrl", [128, NB], F32R)
        lnw = sb("lnw", [128, 2])
        wmh = sb("wmh", [128, 2 * PAIRS * PAIR_W], F32R)
        wml = sb("wml", [128, 2 * PAIRS * PAIR_W], F32R)
        w2 = sb("w2", [128, 3 * PAIRS, D])
        wo = sb("wo", [128, D])

        hx_store = nc.dram_tensor("hx_store", (TP, IMAGES, 2 * NT * D), F32, kind="Internal").ap()
        gacc = sb("gacc", [D + 1, 2, D])
        gtmp = sb("gtmp", [D + 1, 2, D])

        pv = sb("pv", [128, TOK])
        patch = pv[0:D + 1, :]
        hx = sb("hx", [TP, 2, NT, D])
        h_in, x1 = hx[:, 0, :, :], hx[:, 1, :, :]
        hx_row = hx[:].rearrange("p a t f -> p (a t f)")
        xt = sb("xt", [D + 1, TOK])
        at = sb("at", [D + 1, TOK])
        a1 = sb("a1", [TP, NT, D + 2])
        ke = sb("ke", [TP, NT, D + 2])
        tm = [sb(f"tm{n}", [TP, NT, D]) for n in range(6)]
        xc, sq, sg, si, sp1, sp2 = tm
        dp = sb("dp", [TP, NT, D])
        dz = sb("dz", [TP, NT, D])
        dz1 = sb("dz1", [TP, NT, D])
        st = sb("st", [TP, 8, NT])
        h2, x2, res = dp, dz1, dz
        h2_held, x2_held = sb("h2_held", [TP, NT, D]), sb("x2_held", [TP, NT, D])
        rest = sb("rest", [TP, NT, D])
        sq2 = sb("sq2", [TP, NT, D])
        st2 = sb("st2", [TP, 8, NT])
        xd2 = sb("xd2", [TP, NT, 2, D])
        xd = sb("xd", [TP, NT, 2, D])
        xh = sb("xh", [128, TOK], F32R)
        xs = sb("xs", [128, TOK], F32R)
        xm = sb("xm", [128, TOK], F32R)
        xmh = sb("xmh", [128, TOK], F32R)
        qk = sb("qk", [QK, TOK])
        qkh = sb("qkh", [QK, TOK], F32R)
        qkl = sb("qkl", [QK, TOK], F32R)
        qx = sb("qx", [Q_ROWS, NH, TOK], F32R)
        kx = sb("kx", [Q_ROWS, NKV, TOK], F32R)
        v1 = sb("v1", [TP, NT, NKV, 32])
        mx2 = sb("mx2", [TP, NT - 4, NH])
        mx = sb("mx", [TP, NT, 32])
        pt = sb("pt", [128, 2, NH, TOK])
        mraw = pt[:].rearrange("p a h n -> p (a h n)")[:, 0:2 * PAIRS * PAIR_W]
        rden = sb("rden", [TP, NT, NH])
        ke2 = sb("ke2", [TP, NT, D + 2])
        yn = sb("yn", [128, TOK])
        qk_sin = yn[0:QK, :]
        rt = sb("rt", [TP, 8, NT, NE])
        wt = sb("wt", [TP, NT, 40])
        wth = xmh[0:40, :]
        wts = sb("wts", [40, TOK], F32R)
        bw = sb("bw", [128, 2, 448])
        su = sb("su", [128, 2, 448])
        hh = sb("hh", [128, 2, 3, 448])
        zz = sb("zz", [128, 2, 448])
        zacc = sb("zacc", [128, TOK])

        rows = lambda buf, k: buf[0:TP, k, :].rearrange("p (t f) -> p t f", f=D)
        ext = lambda buf: buf[0:TP, 0:NT * (D + 2)].rearrange("p (t f) -> p t f", f=D + 2)
        hx_b = zz[0:TP].rearrange("p a n -> p (a n)")
        cols = lambda buf: buf[0:D + 1].rearrange("p t a f -> p (t a f)")[:, 0:TOK]
        IM = []
        for s in range(2):
            hid = [hh[0:TP, k // 3, k % 3, :].rearrange("p (t f) -> p t f", f=D) for k in range(6)]
            IM.append(Image(
                patch=(patch, yn[0:D + 1, :])[s], hx_row=(hx_row, hx_b)[s],
                h=(h_in, hx_b[:, 0:NT * D].rearrange("p (t f) -> p t f", f=D))[s],
                x1=(x1, hx_b[:, NT * D:].rearrange("p (t f) -> p t f", f=D))[s],
                xt=(xt[:], cols(xd))[s], at=(at[:], cols(xd2))[s],
                a1=(a1[:], ext(zacc))[s], ke=(ke[:], ke2[:])[s],
                xc=(xc[:], hid[0])[s], sq=(sq[:], hid[1])[s], sg=(sg[:], hid[2])[s], si=(si[:], hid[3])[s],
                sp1=(sp1[:], hid[4])[s], sp2=(sp2[:], hid[5])[s], dp=(dp[:], rows(su, 0))[s],
                dz=(dz[:], rows(su, 1))[s], dz1=(dz1[:], rows(bw, 0))[s], st=(st, st2)[s], bank=4 * s))

        P = ctx.enter_context(nc.psum_tensor("P", [128, 8, BANK], F32))
        flat = P[:, :, :].rearrange("p b n -> p (b n)")

        def tiles(b):
            return P[0:TP, b, 0:NT * D].rearrange("p (t f) -> p t f", f=D)

        def tok_cols(c):
            t0, t1 = CHUNKS[c]
            return slice(t0 * TP, t1 * TP)

        def width(c):
            return (CHUNKS[c][1] - CHUNKS[c][0]) * TP

        def is_image(i, which):
            return isinstance(i, int) and i == which

        def in_turn(order, **stages):
            for name in order:
                next(stages[name], None)
            for stage in stages.values():
                for _ in stage:
                    pass

        def second_pass(eng, memory, prepare, maxima, scores, after, route, experts, finish):
            none = lambda: iter(())
            in_scores = "sfsmssmsmmmrsmrsmrrsrssrsrsrs"
            in_experts = ("eaeaepaeaepepeapepeeppemmemmemeemememmemememmememmememmememe"
                          "meemmemememem")

            def round_(i, first=False, second=False, last=False):
                in_turn(in_scores, s=scores(i), f=none() if first or second else finish(i - 2),
                        m=none() if last else memory(i + 1), r=none() if first else route(i - 1))
                in_turn(in_experts, e=none() if first else experts(i - 1), a=after(i),
                        p=none() if last else prepare(i + 1), m=none() if last else maxima(i + 1))

            for stage in (memory, prepare, maxima):
                in_turn("", only=stage(0))
            round_(0, first=True)
            round_(1, second=True)
            with eng.Fori(2, IMAGES - 1) as i:
                round_(i)
            round_(IMAGES - 1, last=True)
            in_turn("", only=finish(IMAGES - 2))
            for stage in (route, experts, finish):
                in_turn("", only=stage(IMAGES - 1))

        names = """loaded later_loaded weights_scaled high_parts set_done weights_split wz0_ps wproj_ready dve_steps
            nws_ready wz_ps wqproj_ready hx_back hx_free pre_ps ar_ready a1_used
            xd_ready xd_ps xh_ready xs_ready qk_ps v_saved rope_done qkh_ready qkl_ready spread_ps qx_zero
            smax_ps smax_read max_ready mxt_ps mrow_act mrow_dve st_ps exp_done diag_done pv_ps pv_saved den_ps
            yn_ready rden_ready rdent_ps wo_ps logit_ps logit_read exp_r wt_ready wt_ps wth_ready wts_ready bw_ps
            bw_saved h1_ps h3_ps hh_ready y_ps z_ready z_added fold_ps out_ready out_sent
            pool_set waited tanh_z tanh_z2 rope_read rows0_ready rows1_ready held
            post_steps pre_steps route_steps z2_used wo_used rest_ready
            rstd_post rstd_pre silu_done var_post var_pre xd2_ps xd2_ready xm_ready xmh_ready""".split()
        S = {n: sem(n) for n in names}
        in_first = """patch_in patch_used h_ps h_saved var_ready rstd_ready x1_ready hx_stored xt_ps xt_ready proj_ps
            keys_saved alr_ready si1_ready slope1_ready a1_ready values_read z2_ps sig2 si2_ready
            dz2_ready da_ps dz1_ready grad_ps dve_steps grads_summed pool_steps""".split()
        S1 = [{n: sem(f"{n}_{s}") for n in in_first} for s in range(2)]

        def first_pass(eng, forward, backward):
            rounds = IMAGES // 2

            in_turn("", only=forward(0, 0))
            in_turn("bf" * 5, b=backward(0, 0), f=forward(0, 1))
            with eng.Fori(1, rounds) as r:
                in_turn("fb" * 5, f=forward(r, 0), b=backward(r - 1, 1))
                in_turn("bf" * 5, b=backward(r, 0), f=forward(r, 1))
            in_turn("", only=backward(rounds - 1, 1))

        block = ctx.enter_context(nc.Block())

        D1, D_FORWARD, D_MEMORY, D_AFTER, D_ROUTER = 9, 5, 10, 3, 21

        SPLIT = ((araw, wah, wal, 0), (rraw, wrh, wrl, 1), (mraw, wmh, wml, 1))
        FIRST_LOADS = ((con[:], A["con"]), (tokw[:], A["tokw"]), (wk_t[:], A["wk_t"]), (ws[:], A["ws"]),
                       (wproj[:, 64:193], A["wproj"]), (w1l_t[:], A["w1l_t"]))
        LATER_LOADS = ((rope[:], A["rope"]), (wq_t[:], A["wq_t"]), (wqproj[:, D:], A["wqp"]),
                       (araw[0:64, :], A["attnw"]), (araw[64:128, :], A["attnw"]),
                       (rraw[0:64, :], A["router"]), (rraw[64:128, :], A["router"]),
                       (lnw[0:64, :], A["lnw"]), (lnw[64:128, :], A["lnw"]),
                       (mraw[0:64], A["w13"]), (mraw[64:128], A["w13"]), (w2[:], A["w2"]), (wo[:], A["wo"]))

        @block.sync
        def _(sp):
            def patches_in(r, s):
                sp.wait_ge(S1[s]["patch_used"], r + 1)
                sp.dma_start(IM[s].patch[0:D, :],
                             A["patches"][:, bass.ds((2 * r + s) * TOK, TOK)]).then_inc(S1[s]["patch_in"], 16)

            def hx_out(r, s):
                sp.wait_ge(S1[s]["x1_ready"], r + 1)
                sp.dma_start(hx_store[:, bass.ds(2 * r + s, 1), :].rearrange("p a n -> p (a n)"),
                             IM[s].hx_row).then_inc(S1[s]["hx_stored"], 16)

            for dst, src in FIRST_LOADS:
                sp.dma_start(dst, src).then_inc(S["loaded"], 16)
            for s in range(2):
                patches_in(0, s)
            for dst, src in LATER_LOADS:
                sp.dma_start(dst, src).then_inc(S["later_loaded"], 16)
            with sp.Fori(0, IMAGES // 2 - 1) as r:
                for s in range(2):
                    hx_out(r, s)
                    patches_in(r + 1, s)
            for s in range(2):
                hx_out(IMAGES // 2 - 1, s)
            for s in range(2):
                sp.wait_ge(S1[s]["hx_stored"], 16 * (IMAGES // 2) + 16)

            def hx_in(i):
                sp.wait_ge(S["hx_free"], i + 1)
                sp.dma_start(hx_row,
                             hx_store[:, bass.ds(i, 1), :].rearrange("p a n -> p (a n)")).then_inc(S["hx_back"], 16)

            def result_out(i):
                sp.wait_ge(S["out_ready"], i + 2)
                sp.dma_start(A["out"][:, bass.ds(i * NT, NT), :], res[:]).then_inc(S["out_sent"], 16)

            for i in range(4):
                hx_in(i)
            with sp.Fori(0, IMAGES - 4) as i:
                result_out(i)
                hx_in(i + 4)
            for i in range(IMAGES - 4, IMAGES):
                result_out(i)
            sp.wait_ge(S["out_sent"], 16 * IMAGES + 16)


        @block.gpsimd
        def _(pool):
            setting = Steps(pool, S["pool_set"])
            settings = [(v1[:], 0.0), (mx[:], 0.0), (wt[:], 0.0), (gacc[:], 0.0),
                        (kx[64:96, :, :].bitcast(F32), 1.0), (wproj[:, 193:194], 0.0),
                        (v1[:, :, :, HD:HD + 1], 1.0)]
            for m in IM:
                settings += [(m.patch[D:D + 1, :], 1.0), (m.xt[D:D + 1, :], 1.0), (m.at[D:D + 1, :], 1.0),
                             (m.a1[:, :, D:], 1.0), (m.ke[:, :, D:], 1.0)]
            for ap, value in settings:
                setting.link(nc.gpsimd.memset(ap, value))
            pool.drain().then_inc(S["set_done"], 1)
            pool.wait_ge(S["loaded"], 16 * len(FIRST_LOADS))
            half = con[0:TP, C_HALF:C_HALF + NT]

            def forward(r, s):
                m, S = IM[s], S1[s]
                pool.wait_ge(S["var_ready"], r + 1)
                nc.gpsimd.tensor_tensor(m.st[:, 3, :], m.st[:, 2, :], half, ALU.pow).then_inc(S["rstd_ready"], 1)
                yield
                yield
                pool.wait_ge(S["si1_ready"], r + 1)
                nc.gpsimd.tensor_tensor(m.sp1, m.si, m.sg, ALU.mult).then_inc(S["pool_steps"], 1)
                nc.gpsimd.tensor_tensor(m.sq, m.si, m.sg, ALU.add).then_inc(S["pool_steps"], 1)
                pool.wait_ge(S["pool_steps"], 2 + 2 * r)
                nc.gpsimd.tensor_tensor(m.sp1, m.sq, m.sp1, ALU.subtract).then_inc(S["slope1_ready"], 1)
                yield

            def backward(r, s):
                yield

            first_pass(pool, forward, backward)

            def rstd(stats, asked, given, count):
                pool.wait_ge(S[asked], count)
                nc.gpsimd.tensor_tensor(stats[:, 3, :], stats[:, 2, :], half, ALU.pow).then_inc(S[given], 1)
                pool.wait_ge(S[given], count)

            def memory(i):
                for k in range(4):
                    yield
                rstd(st, "var_pre", "rstd_pre", 2 * i + 1)
                yield
                rstd(st, "var_pre", "rstd_pre", 2 * i + 2)
                yield

            def prepare(i):
                pool.wait_ge(S["xd_ps"], 2 * i + 1)
                pool.sem_inc(S["waited"], 1)
                nc.gpsimd.memset(qx[64:96, :, :].bitcast(F32), 0.0).then_inc(S["qx_zero"], 1)
                pool.wait_ge(S["qx_zero"], i + 1)
                yield

            def maxima(i):
                yield

            def scores(i):
                yield
                for n, (kb, q0, q1) in enumerate(PIECES):
                    if q0 == kb * TP:
                        for hp in range(2):
                            pool.wait_ge(S["exp_done"], i * 22 + 2 * n + hp + 1)
                            pool.sem_inc(S["waited"], 1)
                            d = pt[0:TP, kb % 2, 2 * hp:2 * hp + 2, kb * TP:(kb + 1) * TP]
                            nc.gpsimd.affine_select(out=d, in_=d, compare_op=ALU.is_ge, fill=0.0, base=0,
                                                    pattern=[[0, 2], [1, TP]], channel_multiplier=-1
                                                    ).then_inc(S["diag_done"], 1)
                    yield

            def after(i):
                for k in range(3):
                    yield
                rstd(st2, "var_post", "rstd_post", i + 1)
                yield

            def route(i):
                yield

            def finish(i):
                yield

            def experts(j):
                for n in range(27):
                    if n % 3 == 2 and n > 2:
                        g = n // 3 - 1
                        c, p = g // PAIRS, g % PAIRS
                        w, cols = width(c), tok_cols(c)
                        if p == 0:
                            yield
                            continue
                        pool.wait_ge(S["z_ready"], 8 * j + g + 1)
                        before = zz[:, 0, 0:w] if p == 1 else zacc[:, cols]
                        ins = nc.gpsimd.tensor_tensor(zacc[:, cols], before, zz[:, g % 2, 0:w], ALU.add)
                        ins.then_inc(S["z_added"], 2 if p == 1 else 1)
                        pool.wait_ge(S["z_added"], 8 * j + g + 1)
                    yield

            second_pass(pool, memory, prepare, maxima, scores, after, route, experts, finish)

        @block.tensor
        def _(pe):
            mm = nc.tensor.matmul

            def transposes(src, rows, b, ready):
                pe.sem_inc(S["waited"], 1)
                for c, (t0, t1) in enumerate(CHUNKS):
                    for t in range(t0, t1):
                        last = nc.tensor.transpose(P[0:rows, b + c, (t - t0) * TP:(t - t0 + 1) * TP],
                                                   src(t), ident[0:TP, 0:TP])
                    last.then_inc(ready, 1)

            pe.wait_ge(S["loaded"], 16 * len(FIRST_LOADS))
            pe.wait_ge(S["set_done"], 1)
            mm(P[0:D, 0, 0:D], wk_t[:], ws[0:D, 0, :], start=True, stop=True).then_inc(S["wz0_ps"], 1)
            pe.wait_ge(S["wproj_ready"], 1)

            tile = lambda t: slice(t * TP, (t + 1) * TP)

            def tiled(b, lhs, rhs, ready):
                for t in range(NT):
                    last = mm(P[0:TP, b, t * D:(t + 1) * D], lhs(t), rhs, start=True, stop=True)
                last.then_inc(ready, 1)

            def forward(r, s):
                m, S = IM[s], S1[s]
                b = m.bank
                pe.wait_ge(S["patch_in"], 16 * r + 16)
                pe.wait_ge(S["grads_summed"], r + 1)
                tiled(b, lambda t: m.patch[:, tile(t)], tokw[:], S["h_ps"])
                yield
                yield
                pe.wait_ge(S["x1_ready"], r + 1)
                transposes(lambda t: m.x1[:, t, :], D, b, S["xt_ps"])
                yield
                pe.wait_ge(S["xt_ready"], 6 * r + 2)
                for t in range(NT):
                    o = b * BANK + t * 256
                    last = mm(flat[0:TP, o:o + 194], m.xt[:, tile(t)], wproj[:], start=True, stop=True)
                last.then_inc(S["proj_ps"], 1)
                yield
                pe.wait_ge(S["values_read"], r + 1)
                transposes(lambda t: m.a1[:, t, 0:D], D, b, S["xt_ps"])
                yield

            def backward(r, s):
                m, S = IM[s], S1[s]
                b = m.bank
                pe.wait_ge(S["xt_ready"], 6 * r + 4)
                tiled(b + 2, lambda t: m.at[:, tile(t)], ws[:, 1, :], S["z2_ps"])
                yield
                pe.wait_ge(S["dz2_ready"], r + 1)
                transposes(lambda t: m.dz[:, t, :], D, b, S["xt_ps"])
                for t in range(NT):
                    mm(P[0:D + 1, b + 3, 256 + D:256 + 2 * D], m.a1[:, t, 0:D + 1], m.dz[:, t, :],
                       start=(t == 0), stop=(t == NT - 1))
                yield
                pe.wait_ge(S["xt_ready"], 6 * r + 6)
                tiled(b + 2, lambda t: m.xt[0:D, tile(t)], w1l_t[:], S["da_ps"])
                yield
                pe.wait_ge(S["dz1_ready"], r + 1)
                pe.wait_ge(S["keys_saved"], r + 1)
                for t in range(NT):
                    last = mm(P[0:D + 1, b + 3, 256:256 + D], m.ke[:, t, 0:D + 1], m.dz1[:, t, :],
                              start=(t == 0), stop=(t == NT - 1))
                last.then_inc(S["grad_ps"], 1)
                yield

            first_pass(pe, forward, backward)
            pe.wait_ge(S["later_loaded"], 16 * len(LATER_LOADS))
            pe.wait_ge(S["nws_ready"], 1)
            mm(P[0:D, 0, 0:D], wq_t[:], nws[0:D, 0, :], start=True, stop=True).then_inc(S["wz_ps"], 1)
            pe.wait_ge(S["wqproj_ready"], 1)
            pe.sem_inc(S["hx_free"], 1)

            def turned(src):
                return lambda t: src[:, t, :, :].rearrange("p a f -> p (a f)")

            def memory(i):
                pe.wait_ge(S["hx_back"], 16 * i + 16)
                transposes(lambda t: x1[:, t, :], D, 4, S["pre_ps"])
                yield
                pe.wait_ge(S["ar_ready"], 4 * i + 2)
                for t in range(NT):
                    last = mm(flat[0:TP, 4 * BANK + t * 128:4 * BANK + t * 128 + 128], xt[:, t * TP:(t + 1) * TP],
                              wqproj[:], start=True, stop=True)
                last.then_inc(S["pre_ps"], 1)
                yield
                pe.wait_ge(S["a1_used"], i + 1)
                transposes(lambda t: a1[:, t, 0:D], D, 4, S["pre_ps"])
                yield
                pe.wait_ge(S["ar_ready"], 4 * i + 4)
                tiled(4, lambda t: at[:, t * TP:(t + 1) * TP], nws[:, 1, :], S["pre_ps"])
                yield
                pe.wait_ge(S["z2_used"], i + 1)
                yield

            def prepare(i):
                pe.wait_ge(S["xd_ready"], i + 1)
                if not is_image(i, 0):
                    pe.wait_ge(S["yn_ready"], 2 * i)
                transposes(turned(xd), 128, 0, S["xd_ps"])
                yield
                pe.wait_ge(S["xs_ready"], 2 * i + 2)
                if is_image(i, 0):
                    pe.wait_ge(S["weights_split"], 1)
                if not is_image(i, 0):
                    pe.wait_ge(S["wo_used"], i)
                for c in range(2):
                    if c == 1:
                        pe.wait_ge(S["rope_read"], 2 * i + 1)
                    for k in range(2):
                        for w in (wah, wal):
                            last = mm(P[0:QK, k, 0:width(c)], w[:, k * QK:(k + 1) * QK],
                                      xs[:, tok_cols(c)], start=(w is wah), stop=(w is wal))
                    last.then_inc(S["qk_ps"], 1)
                    yield
                pe.wait_ge(S["rope_read"], 2 * i + 2)
                for t in range(NT):
                    for w in (wah, wal):
                        last = mm(P[0:TP, 0, t * 32:(t + 1) * 32], xs[:, t * TP:(t + 1) * TP], w[:, 2 * QK:],
                                  start=(w is wah), stop=(w is wal))
                last.then_inc(S["qk_ps"], 1)
                yield
                pe.wait_ge(S["qkl_ready"], i + 1)
                pe.wait_ge(S["v_saved"], i + 1)
                for o in range(3):
                    for c in range(2):
                        if o:
                            pe.wait_ge(S["rows0_ready" if c == 0 else "rows1_ready"], 3 * i + o)
                        mm(P[:, c, 0:width(c)], sel[0:QK, o, :], qkh[:, tok_cols(c)], start=True, stop=False)
                        mm(P[:, c, 0:width(c)], sel[0:QK, 3 + o, :], qkl[:, tok_cols(c)], start=False,
                           stop=True).then_inc(S["spread_ps"], 1)
                    yield

            def maxima(i):
                pe.wait_ge(S["qx_zero"], i + 1)
                pe.wait_ge(S["rows0_ready"], 3 * i + 3)
                pe.wait_ge(S["rows1_ready"], 3 * i + 3)
                f = 0
                for qt in range(NT):
                    for h in range(NH):
                        keys = (qt + 1) * TP
                        for k0 in range(0, keys, BANK):
                            if f >= 2:
                                pe.wait_ge(S["smax_read"], FILLS * i + f - 1)
                            k1 = min(keys, k0 + BANK)
                            diag = max(k0, qt * TP)
                            o = (f % 2) * BANK - k0
                            last = mm(flat[0:TP, o + k0:o + k1], qx[:, h, qt * TP:keys], kx[:, h // 2, k0:k1],
                                      start=True, stop=diag >= k1)
                            if diag < k1:
                                last = mm(flat[0:TP, o + diag:o + k1], idb[:],
                                          maskb[:, diag - qt * TP:k1 - qt * TP], start=False, stop=True)
                            last.then_inc(S["smax_ps"], 1)
                            f += 1
                        if qt >= 4 or h % 2:
                            yield

            def scores(i):
                pe.wait_ge(S["max_ready"], i + 1)
                for c, (t0, t1) in enumerate(CHUNKS):
                    for t in range(t0, t1):
                        last = mm(P[64:96, c, (t - t0) * TP:(t - t0 + 1) * TP], mx[:, t, :], ident[0:TP, 0:TP],
                                  start=True, stop=True)
                    last.then_inc(S["mxt_ps"], 1)
                yield
                pe.wait_ge(S["mrow_act"], 4 * i + 4)
                pe.wait_ge(S["mrow_dve"], 4 * i + 4)

                def weights(n):
                    kb, q0, q1 = PIECES[n]
                    for hp in range(2):
                        m = 2 * n + hp
                        if m >= 2:
                            pe.wait_ge(S["exp_done"], 22 * i + m - 1)
                        for j in range(2):
                            last = mm(P[0:TP, (m % 2) * 2 + j, 0:q1 - q0], kx[:, hp, kb * TP:(kb + 1) * TP],
                                      qx[:, 2 * hp + j, q0:q1], start=True, stop=True)
                        last.then_inc(S["st_ps"], 1)

                def values(n):
                    kb, q0, q1 = PIECES[n]
                    pe.wait_ge(S["exp_done"], 22 * i + 2 * n + 2)
                    if q0 == kb * TP:
                        pe.wait_ge(S["diag_done"], 14 * i + 2 * kb + 2)
                    c = q0 >= 448
                    for h in range(NH):
                        last = mm(P[32 * h:32 * h + 32, 6 + c, q0 - 448 * c:q1 - 448 * c], v1[:, kb, h // 2, :],
                                  pt[0:TP, kb % 2, h, q0:q1], start=(kb == 0), stop=(kb == (6 if c else 3)))
                    last.then_inc(S["pv_ps"], 1)

                weights(0)
                yield
                if not is_image(i, 0):
                    pe.wait_ge(S["out_ready"], i)
                for n in range(1, len(PIECES) + 1):
                    if n < len(PIECES):
                        weights(n)
                    values(n - 1)
                    yield

            def after(i):
                pe.wait_ge(S["pv_saved"], 2 * i + 2)
                for t in range(NT):
                    last = mm(P[0:TP, 0, t * NH:(t + 1) * NH], pv[:, t * TP:(t + 1) * TP],
                              con[:, C_DEN:C_DEN + NH], start=True, stop=True)
                last.then_inc(S["den_ps"], 1)
                yield
                pe.wait_ge(S["rden_ready"], i + 1)
                transposes(turned(xd2), 128, 0, S["rdent_ps"])
                yield
                pe.wait_ge(S["yn_ready"], 2 * i + 2)
                if not is_image(i, IMAGES - 1):
                    pe.wait_ge(S["xs_ready"], 2 * i + 4)
                tiled(0, lambda t: yn[:, t * TP:(t + 1) * TP], wo[:], S["wo_ps"])
                yield

            def route(i):
                pe.wait_ge(S["xd2_ready"], i + 1)
                transposes(turned(xd2), 128, 4, S["xd2_ps"])
                yield
                pe.wait_ge(S["xm_ready"], 2 * i + 2)
                for t in range(NT):
                    for w in (wrh, wrl):
                        last = mm(P[0:TP, 4, t * NE:(t + 1) * NE], xm[:, t * TP:(t + 1) * TP], w[:],
                                  start=(w is wrh), stop=(w is wrl))
                last.then_inc(S["logit_ps"], 1)
                for k in range(4):
                    yield
                pe.wait_ge(S["wt_ready"], i + 1)
                transposes(lambda t: wt[:, t, :], 40, 4, S["wt_ps"])
                yield
                yield

            def experts(j):
                def up(n):
                    c, p, k = n // 12, n // 3 % 4, n % 3
                    m = TAIL_W if k == 2 else MAIN
                    for b, ready, freed in ((2, "h1_ps", "silu_done"), (4, "h3_ps", "hh_ready")):
                        if n >= 2:
                            pe.wait_ge(S[freed], 24 * j + n - 1)
                        elif n == 0 and b == 4:
                            pe.wait_ge(S["wts_ready"], 2 * j + 2)
                        o = p * PAIR_W + k * MAIN + (b // 4) * PAIRS * PAIR_W
                        for w in (wmh, wml):
                            last = mm(P[0:m, b + n % 2, 0:width(c)], w[:, o:o + m], xm[:, tok_cols(c)],
                                      start=(w is wmh), stop=(w is wml))
                        last.then_inc(S[ready], 1)

                def down(g):
                    c, p = g // 4, g % 4
                    w = width(c)
                    if g >= 1:
                        pe.wait_ge(S["bw_saved"], 8 * j + g)
                    mm(P[:, 7, 0:w], selp[:, p, :], wts[:, tok_cols(c)], start=True,
                       stop=True).then_inc(S["bw_ps"], 1)
                    pe.wait_ge(S["hh_ready"], 24 * j + 3 * g + 3)
                    if g >= 1:
                        pe.wait_ge(S["z_ready"], 8 * j + g)
                    for e in range(2):
                        mm(P[64 * e:64 * e + 64, 6, 0:w], w2[:, 3 * p + e, :], hh[:, g % 2, e, 0:w], start=True,
                           stop=False)
                    for e in range(2):
                        last = mm(P[64 * e:64 * e + 64, 6, 0:w], w2[64 * e:64 * e + TAIL, 3 * p + 2, :],
                                  hh[64 * e:64 * e + TAIL, g % 2, 2, 0:w], start=False, stop=True)
                    last.then_inc(S["y_ps"], 1)

                for n in range(26):
                    if n < 24:
                        up(n)
                    if n % 3 == 1 and n > 1:
                        down(n // 3 - 1)
                    yield

            def finish(j):
                pe.wait_ge(S["z_added"], 8 * j + 8)
                for t in range(NT):
                    last = mm(P[0:TP, 6, t * D:(t + 1) * D], zacc[:, t * TP:(t + 1) * TP],
                              con[:, C_FOLD:C_FOLD + 64], start=True, stop=True)
                last.then_inc(S["fold_ps"], 1)
                yield

            second_pass(pe, memory, prepare, maxima, scores, after, route, experts, finish)

        @block.scalar
        def _(act):
            copy = lambda out, in_: nc.scalar.activation(out, in_, ACT.Copy)

            def evacuate(dst, rows, b, ps, ready, i, per, n, S=S):
                for c in range(2):
                    act.wait_ge(S[ps], i * per + n + c)
                    copy(dst[0:rows, tok_cols(c)], P[0:rows, b + c, 0:width(c)]).then_inc(S[ready], 1)

            act.wait_ge(S["set_done"], 1)

            def forward(r, s):
                m, S = IM[s], S1[s]
                b = m.bank
                act.wait_ge(S["h_ps"], r + 1)
                act.wait_ge(S["hx_stored"], 16 * r + 16)
                copy(m.h, tiles(b)).then_inc(S["h_saved"], 1)
                yield
                yield
                evacuate(m.xt, D, b, "xt_ps", "xt_ready", r, 6, 1, S)
                yield
                act.wait_ge(S["proj_ps"], r + 1)
                pr = flat[0:TP, b * BANK:b * BANK + NT * 256].rearrange("p (t f) -> p t f", f=256)
                nc.scalar.activation(m.sg, pr[:, :, 0:D], ACT.Sigmoid)
                copy(m.ke[:, :, 0:D], pr[:, :, D:2 * D]).then_inc(S["keys_saved"], 1)
                nc.scalar.activation(m.st[:, 4, :], pr[:, :, 192], ACT.Sigmoid).then_inc(S["alr_ready"], 1)
                yield
                evacuate(m.at, D, b, "xt_ps", "xt_ready", r, 6, 3, S)
                yield

            def backward(r, s):
                m, S = IM[s], S1[s]
                b = m.bank
                act.wait_ge(S["z2_ps"], r + 1)
                act.wait_ge(S["slope1_ready"], r + 1)
                nc.scalar.activation(m.sg, tiles(b + 2), ACT.Sigmoid).then_inc(S["sig2"], 1)
                yield
                evacuate(m.xt, D, b, "xt_ps", "xt_ready", r, 6, 5, S)
                yield

            first_pass(act, forward, backward)
            act.wait_ge(S["later_loaded"], 16 * len(LATER_LOADS))
            for n, (raw, high, low, ln) in enumerate(SPLIT):
                nc.scalar.activation(raw[:], raw[:], ACT.Copy, scale=lnw[:, ln:ln + 1]).then_inc(S["weights_scaled"], 1)
                act.wait_ge(S["weights_scaled"], n + 1)
                copy(high[:], raw[:]).then_inc(S["high_parts"], 1)

            def memory(i):
                evacuate(xt, D, 4, "pre_ps", "ar_ready", i, 6, 1)
                yield
                act.wait_ge(S["pre_ps"], 6 * i + 3)
                zq = flat[0:TP, 4 * BANK:4 * BANK + NT * 128].rearrange("p (t f) -> p t f", f=128)
                nc.scalar.activation(sg[:], zq[:, :, 0:D], ACT.Tanh, scale=0.5).then_inc(S["tanh_z"], 1)
                yield
                evacuate(at, D, 4, "pre_ps", "ar_ready", i, 6, 4)
                yield
                act.wait_ge(S["pre_ps"], 6 * i + 6)
                nc.scalar.activation(sg[:], tiles(4), ACT.Tanh, scale=0.5).then_inc(S["tanh_z2"], 1)
                yield

            def spread_rows(o, c):
                dst, first = kx if o == 2 else qx, 0 if o == 2 else 2 * o
                copy(dst[0:64, first, tok_cols(c)], P[0:64, c, 0:width(c)])
                return copy(dst[0:64, first + 1, tok_cols(c)], P[64:128, c, 0:width(c)])

            def prepare(i):
                evacuate(xh, 128, 0, "xd_ps", "xh_ready", i, 2, 1)
                yield
                yield
                yield
                act.wait_ge(S["qk_ps"], 3 * i + 3)
                v = P[0:TP, 0, 0:NT * 32].rearrange("p (t g d) -> p t g d", g=NKV, d=HD)
                for g in range(NKV):
                    last = copy(v1[:, :, g, 0:HD], v[:, :, g, :])
                last.then_inc(S["v_saved"], 1)
                act.wait_ge(S["rope_done"], i + 1)
                copy(qkh[:], qk[:]).then_inc(S["qkh_ready"], 1)
                yield
                for o in range(3):
                    for c, taken in enumerate(("rows0_ready", "rows1_ready")):
                        act.wait_ge(S["spread_ps"], 6 * i + 2 * o + c + 1)
                        spread_rows(o, c).then_inc(S[taken], 1)
                    yield

            def maxima(i):
                yield

            def scores(i):
                act.wait_ge(S["mxt_ps"], 2 * i + 1)
                for h in range(NH):
                    nc.scalar.activation(qx[64:96, h, tok_cols(0)], P[64:96, 0, 0:width(0)], ACT.Copy,
                                         scale=con[64:96, C_MAXROW + h:C_MAXROW + h + 1]
                                         ).then_inc(S["mrow_act"], 1)
                yield
                for n, (kb, q0, q1) in enumerate(PIECES):
                    if kb >= 2:
                        act.wait_ge(S["pv_ps"], 11 * i + first_piece(kb - 1))
                    for hp in range(2):
                        m = 2 * n + hp
                        act.wait_ge(S["st_ps"], 22 * i + m + 1)
                        b = (m % 2) * 2
                        nc.scalar.activation(pt[0:TP, kb % 2, 2 * hp:2 * hp + 2, q0:q1],
                                             P[0:TP, b:b + 2, 0:q1 - q0], ACT.Exp,
                                             scale=float(HD) ** -0.5).then_inc(S["exp_done"], 1)
                    yield
                act.wait_ge(S["pv_ps"], 11 * i + 11)
                for c in range(2):
                    copy(pv[:, tok_cols(c)], P[:, 6 + c, 0:width(c)]).then_inc(S["pv_saved"], 1)

            def after(i):
                yield

            def route(i):
                evacuate(xmh, 128, 4, "xd2_ps", "xmh_ready", i, 2, 1)
                yield
                act.wait_ge(S["logit_read"], i + 1)
                nc.scalar.activation(rt[:, 1, :, :], rt[:, 0, :, :], ACT.Exp).then_inc(S["exp_r"], 1)
                for k in range(4):
                    yield
                evacuate(wth, 40, 4, "wt_ps", "wth_ready", i, 2, 1)
                yield

            def finish(i):
                yield

            def experts(j):
                for n in range(26):
                    if n < 24:
                        w = width(n // 12)
                        r = TAIL_W if n % 3 == 2 else MAIN
                        act.wait_ge(S["h1_ps"], 24 * j + n + 1)
                        if n >= 2:
                            act.wait_ge(S["hh_ready"], 24 * j + n - 1)
                        nc.scalar.activation(su[0:r, n % 2, 0:w], P[0:r, 2 + n % 2, 0:w],
                                             ACT.Silu).then_inc(S["silu_done"], 1)
                    if n % 3 == 1 and n > 1:
                        g = n // 3 - 1
                        w = width(g // 4)
                        act.wait_ge(S["bw_ps"], 8 * j + g + 1)
                        if g >= 2:
                            act.wait_ge(S["z_ready"], 8 * j + g - 1)
                        copy(bw[:, g % 2, 0:w], P[:, 7, 0:w]).then_inc(S["bw_saved"], 1)
                    yield

            second_pass(act, memory, prepare, maxima, scores, after, route, experts, finish)

        @block.vector
        def _(dve):
            V = nc.vector
            chain = Steps(dve, S["dve_steps"])
            link = chain.link

            def over_tiles(s, n=D):
                return s.unsqueeze(2).broadcast_to([TP, NT, n])

            def variance(src, centre, var, link, st, sq, xc=None):
                if centre:
                    link(V.reduce_sum(st[:, 0, :], src, axis=AX.X))
                    link(V.scalar_tensor_tensor(xc, over_tiles(st[:, 0, :]), -1.0 / D, src, ALU.mult, ALU.add))
                    src = xc
                link(V.tensor_tensor(sq, src, src, ALU.mult))
                link(V.reduce_sum(st[:, 5, :], sq, axis=AX.X))
                V.tensor_scalar(st[:, 2, :], st[:, 5, :], 1.0 / D, EPS_LN if centre else EPS_RMS, ALU.mult,
                                ALU.add).then_inc(var, 1)

            dve.wait_ge(S["loaded"], 16 * len(FIRST_LOADS))
            dve.wait_ge(S["set_done"], 1)
            V.tensor_copy(sel[:], con[:, C_SELH:C_SELH + 768].rearrange("p (o r) -> p o r", o=6))
            V.tensor_copy(selp[:], con[0:40, C_PAIR:C_PAIR + PAIRS * 128].rearrange("p (o r) -> p o r", o=PAIRS))
            V.tensor_copy(idb[:], con[0:TP, C_ID:C_ID + TP])
            V.tensor_copy(maskb[:], con[0:TP, C_MASK:C_MASK + TP])
            dve.wait_ge(S["wz0_ps"], 1)
            V.tensor_copy(wproj[0:D, 0:D], P[0:D, 0, 0:D])
            V.tensor_copy(wproj[D:D + 1, 0:D], ws[D:D + 1, 0, :]).then_inc(S["wproj_ready"], 1)
            for s in range(2):
                dve.sem_inc(S1[s]["patch_used"], 1)
                dve.sem_inc(S1[s]["hx_stored"], 16)
                dve.sem_inc(S1[s]["grads_summed"], 1)
            dve.sem_inc(S["out_sent"], 16)
            dve.sem_inc(S["out_ready"], 1)
            chains = [Steps(dve, S1[s]["dve_steps"]) for s in range(2)]

            def forward(r, s):
                m, S = IM[s], S1[s]
                chains[s].round(r, D1)
                link, b = chains[s].link, m.bank
                dve.wait_ge(S["h_saved"], r + 1)
                dve.sem_inc(S["patch_used"], 1)
                variance(m.h, True, S["var_ready"], link, m.st, m.sq, m.xc)
                yield
                dve.wait_ge(S["rstd_ready"], r + 1)
                V.tensor_tensor(m.x1, m.xc, over_tiles(m.st[:, 3, :]), ALU.mult).then_inc(S["x1_ready"], 1)
                yield
                yield
                pr = flat[0:TP, b * BANK:b * BANK + NT * 256].rearrange("p (t f) -> p t f", f=256)
                dve.wait_ge(S["alr_ready"], r + 1)
                V.tensor_tensor(m.si, pr[:, :, 0:D], m.sg, ALU.mult).then_inc(S["si1_ready"], 1)
                dve.wait_ge(S["si1_ready"], r + 1)
                V.tensor_tensor(m.a1[:, :, 0:D], m.ke[:, :, 0:D], m.si, ALU.add).then_inc(S["a1_ready"], 1)
                dve.wait_ge(S["a1_ready"], r + 1)
                V.tensor_tensor(m.xc, m.a1[:, :, 0:D], pr[:, :, 2 * D:3 * D],
                                ALU.subtract).then_inc(S["values_read"], 1)
                link(V.tensor_scalar(m.st[:, 6, :], m.st[:, 4, :], MAX_ALR * 2.0 / D, None, ALU.mult))
                assert chains[s].n == D_FORWARD, chains[s].n
                yield
                yield

            def backward(r, s):
                m, S = IM[s], S1[s]
                chains[s].round(r, D1, D_FORWARD)
                link, b = chains[s].link, m.bank
                dve.wait_ge(S["sig2"], r + 1)
                V.tensor_tensor(m.si, tiles(b + 2), m.sg, ALU.mult).then_inc(S["si2_ready"], 1)
                dve.wait_ge(S["si2_ready"], r + 1)
                link(V.tensor_tensor(m.xc, m.xc, m.si, ALU.add))
                V.tensor_tensor(m.dp, m.xc, over_tiles(m.st[:, 6, :]), ALU.mult)
                link(V.scalar_tensor_tensor(m.sp2, m.sg, -1.0, m.si, ALU.add, ALU.mult))
                link(V.tensor_tensor(m.sp2, m.sg, m.sp2, ALU.subtract))
                V.tensor_tensor(m.dz, m.dp, m.sp2, ALU.mult).then_inc(S["dz2_ready"], 1)
                yield
                yield
                dve.wait_ge(S["da_ps"], r + 1)
                link(V.tensor_tensor(m.xc, tiles(b + 2), m.dp, ALU.add))
                V.tensor_tensor(m.dz1, m.xc, m.sp1, ALU.mult).then_inc(S["dz1_ready"], 1)
                yield
                dve.wait_ge(S["grad_ps"], r + 1)
                V.tensor_tensor(gacc[:], gacc[:], P[0:D + 1, b + 3, 256:256 + 2 * D].rearrange(
                    "p (l n) -> p l n", l=2), ALU.add).then_inc(S["grads_summed"], 1)
                dve.wait_ge(S["grads_summed"], r + 2)
                assert chains[s].n == D1, chains[s].n
                yield

            first_pass(dve, forward, backward)
            link(V.tensor_scalar(gtmp[:], gacc[:], -1.0, None, ALU.mult))
            link(V.tensor_tensor(gtmp[:], gacc[:], gtmp[:], ALU.max))
            link(V.tensor_scalar(gtmp[:], gtmp[:], EPS_ADAM, None, ALU.add))
            link(V.reciprocal(gtmp[:], gtmp[:]))
            link(V.tensor_tensor(gtmp[:], gacc[:], gtmp[:], ALU.mult))
            link(V.tensor_scalar(gtmp[:], gtmp[:], LR, None, ALU.mult))
            link(V.tensor_scalar(nws[:], ws[:], 1.0 - LR * WD, None, ALU.mult))
            V.tensor_tensor(nws[:], nws[:], gtmp[:], ALU.subtract).then_inc(S["nws_ready"], 1)
            dve.wait_ge(S["nws_ready"], 1)
            dve.wait_ge(S["wz_ps"], 1)
            V.tensor_copy(wqproj[0:D, 0:D], P[0:D, 0, 0:D])
            V.tensor_copy(wqproj[D:D + 1, 0:D], nws[D:D + 1, 0, :]).then_inc(S["wqproj_ready"], 1)
            for n, (raw, high, low, ln) in enumerate(SPLIT):
                dve.wait_ge(S["high_parts"], n + 1)
                last = V.tensor_tensor(low[:], raw[:], high[:].bitcast(F32), ALU.subtract)
            last.then_inc(S["weights_split"], 1)
            rs = lambda k: rt[:, k, :, :]

            def twice(dup, src, stats, ready):
                V.tensor_tensor(dup[:], src.unsqueeze(2).broadcast_to([TP, NT, 2, D]),
                                stats[:, 3, :].unsqueeze(2).unsqueeze(3).broadcast_to([TP, NT, 2, D]),
                                ALU.mult).then_inc(ready, 1)

            def low_parts(dst, high, low, b, given, ready, i):
                r = dst.shape[0]
                for c in range(2):
                    dve.wait_ge(S[given], 2 * i + c + 1)
                    V.scalar_tensor_tensor(dst[:, tok_cols(c)], high[:, tok_cols(c)].bitcast(F32),
                                           con[0:r, low:low + 1], P[0:r, b + c, 0:width(c)], ALU.mult,
                                           ALU.add).then_inc(S[ready], 1)

            pre = Steps(dve, S["pre_steps"])
            post = Steps(dve, S["post_steps"])
            router = Steps(dve, S["route_steps"])

            def memory(i):
                pre.round(i, D_MEMORY)
                yield
                zq = flat[0:TP, 4 * BANK:4 * BANK + NT * 128].rearrange("p (t f) -> p t f", f=128)
                dve.wait_ge(S["tanh_z"], i + 1)
                pre.link(V.scalar_tensor_tensor(sq[:], sg[:], 1.0, zq[:, :, 0:D], ALU.add, ALU.mult))
                V.scalar_tensor_tensor(a1[:, :, 0:D], sq[:], 0.5, zq[:, :, D:], ALU.mult,
                                       ALU.add).then_inc(S["a1_used"], 1)
                dve.wait_ge(S["a1_used"], i + 1)
                pre.link(V.tensor_tensor(h2[:], a1[:, :, 0:D], h_in, ALU.add))
                dve.sem_inc(S["hx_free"], 1)
                yield
                yield
                dve.wait_ge(S["tanh_z2"], i + 1)
                V.scalar_tensor_tensor(sq[:], sg[:], 1.0, tiles(4), ALU.add, ALU.mult).then_inc(S["z2_used"], 1)
                dve.wait_ge(S["z2_used"], i + 1)
                pre.link(V.scalar_tensor_tensor(h2[:], sq[:], 0.5, h2[:], ALU.mult, ALU.add))
                yield
                variance(h2[:], True, S["var_pre"], pre.link, st, sq[:], xc[:])
                yield
                dve.wait_ge(S["rstd_pre"], 2 * i + 1)
                pre.link(V.tensor_tensor(x2[:], xc[:], over_tiles(st[:, 3, :]), ALU.mult))
                variance(x2[:], False, S["var_pre"], pre.link, st, sq[:])
                yield
                dve.wait_ge(S["rstd_pre"], 2 * i + 2)
                twice(xd, x2[:], st, S["xd_ready"])
                assert pre.n == D_MEMORY, pre.n
                yield

            def prepare(i):
                low_parts(xs, xh, C_LOW64, 0, "xh_ready", "xs_ready", i)
                yield
                for c in range(2):
                    dve.wait_ge(S["qk_ps"], 3 * i + c + 1)
                    V.tensor_tensor(qk[:, tok_cols(c)], P[0:QK, 0, 0:width(c)], rope[:, 0, tok_cols(c)], ALU.mult)
                    V.tensor_tensor(qk_sin[:, tok_cols(c)], P[0:QK, 1, 0:width(c)], rope[:, 1, tok_cols(c)],
                                    ALU.mult).then_inc(S["rope_read"], 1)
                    yield
                dve.wait_ge(S["rope_read"], 2 * i + 2)
                V.tensor_tensor(qk[:], qk[:], qk_sin[:], ALU.add).then_inc(S["rope_done"], 1)
                dve.wait_ge(S["qkh_ready"], i + 1)
                V.tensor_tensor(qkl[:], qk[:], qkh[:].bitcast(F32), ALU.subtract).then_inc(S["qkl_ready"], 1)
                yield
                for o in range(3):
                    yield

            def maxima(i):
                f = 0
                for qt in range(NT):
                    for h in range(NH):
                        keys = (qt + 1) * TP
                        for k0 in range(0, keys, BANK):
                            dve.wait_ge(S["smax_ps"], FILLS * i + f + 1)
                            o = (f % 2) * BANK
                            part = mx2[:, qt - 4, h:h + 1] if k0 else mx[:, qt, h:h + 1]
                            V.reduce_max(part, flat[0:TP, o:o + min(keys - k0, BANK)],
                                         axis=AX.X).then_inc(S["smax_read"], 1)
                            f += 1
                        if qt >= 4 or h % 2:
                            yield
                dve.wait_ge(S["smax_read"], FILLS * i + FILLS)
                V.tensor_tensor(mx[:, 4:NT, 0:NH], mx[:, 4:NT, 0:NH], mx2[:], ALU.max).then_inc(S["max_ready"], 1)

            def scores(i):
                dve.wait_ge(S["mxt_ps"], 2 * i + 2)
                for h in range(NH):
                    V.tensor_scalar(qx[64:96, h, tok_cols(1)], P[64:96, 1, 0:width(1)],
                                    con[64:96, C_MAXROW + h:C_MAXROW + h + 1], None,
                                    ALU.mult).then_inc(S["mrow_dve"], 1)
                yield
                if not is_image(i, 0):
                    sum_up(i - 1)
                V.tensor_copy(h2_held[:], h2[:])
                V.tensor_copy(x2_held[:], x2[:]).then_inc(S["held"], 1)
                dve.wait_ge(S["held"], i + 1)
                yield

            rank = con[0:TP, C_RANK:C_RANK + NT * NE].rearrange("p (t e) -> p t e", e=NE)

            def after(i):
                post.round(i, D_AFTER)
                link = post.link
                dve.wait_ge(S["den_ps"], i + 1)
                link(V.reciprocal(rden[:], P[0:TP, 0, 0:NT * NH].rearrange("p (t h) -> p t h", h=NH)))
                V.tensor_copy(xd2[:].rearrange("p t a (b n) -> p t (a b) n", n=32),
                              rden[:].unsqueeze(3).broadcast_to([TP, NT, NH, 32])).then_inc(S["rden_ready"], 1)
                yield
                for c in range(2):
                    dve.wait_ge(S["rdent_ps"], 2 * i + c + 1)
                    V.tensor_tensor(yn[:, tok_cols(c)], pv[:, tok_cols(c)], P[:, c, 0:width(c)],
                                    ALU.mult).then_inc(S["yn_ready"], 1)
                yield
                dve.wait_ge(S["wo_ps"], i + 1)
                V.tensor_tensor(x2_held[:], x2_held[:], tiles(0), ALU.add).then_inc(S["wo_used"], 1)
                dve.wait_ge(S["wo_used"], i + 1)
                yield
                variance(x2_held[:], False, S["var_post"], link, st2, sq2[:])
                yield
                dve.wait_ge(S["rstd_post"], i + 1)
                twice(xd2, x2_held[:], st2, S["xd2_ready"])
                assert post.n == D_AFTER, post.n
                yield

            def sum_up(i):
                V.tensor_tensor(rest[:], h2_held[:], x2_held[:], ALU.add).then_inc(S["rest_ready"], 1)
                dve.wait_ge(S["rest_ready"], i + 1)

            def route(i):
                low_parts(xm, xmh, C_LOW64, 4, "xmh_ready", "xm_ready", i)
                yield
                router.round(i, D_ROUTER)
                link = router.link
                dve.wait_ge(S["logit_ps"], i + 1)
                lg = P[0:TP, 4, 0:NT * NE].rearrange("p (t e) -> p t e", e=NE)
                link(V.reduce_max(st2[:, 0, :], lg, axis=AX.X))
                V.tensor_tensor(rs(0), lg, over_tiles(st2[:, 0, :], NE), ALU.subtract).then_inc(S["logit_read"], 1)
                yield
                dve.wait_ge(S["exp_r"], i + 1)
                link(V.reduce_sum(st2[:, 1, :], rs(1), axis=AX.X))
                link(V.reciprocal(st2[:, 1, :], st2[:, 1, :]))
                link(V.tensor_tensor(rs(1), rs(1), over_tiles(st2[:, 1, :], NE), ALU.mult))
                src = rs(1)
                for k in range(2):
                    link(V.reduce_max(st2[:, 4 + k, :], src, axis=AX.X))
                    link(V.tensor_tensor(rs(3), src, over_tiles(st2[:, 4 + k, :], NE), ALU.is_equal))
                    link(V.tensor_tensor(rs(3), rs(3), rank, ALU.mult))
                    link(V.reduce_max(st2[:, 6, :], rs(3), axis=AX.X))
                    link(V.tensor_tensor(rs(4 + k), rank, over_tiles(st2[:, 6, :], NE), ALU.is_equal))
                    if k == 0:
                        link(V.scalar_tensor_tensor(rs(2), rs(4), -2.0, rs(1), ALU.mult, ALU.add))
                        src = rs(2)
                    yield
                link(V.tensor_tensor(rs(5), rs(5), rs(4), ALU.add))
                link(V.tensor_tensor(rs(1), rs(1), rs(5), ALU.mult))
                link(V.reduce_sum(st2[:, 6, :], rs(1), axis=AX.X))
                link(V.tensor_scalar(st2[:, 6, :], st2[:, 6, :], EPS_TOP, None, ALU.add))
                link(V.reciprocal(st2[:, 6, :], st2[:, 6, :]))
                link(V.tensor_tensor(wt[:, :, 0:NE], rs(1), over_tiles(st2[:, 6, :], NE), ALU.mult))
                V.tensor_copy(wt[:, :, 32:40], wt[:, :, 0:NE]).then_inc(S["wt_ready"], 1)
                yield
                low_parts(wts, wth, C_LOW32, 4, "wth_ready", "wts_ready", i)
                assert router.n == D_ROUTER, router.n
                yield

            def experts(j):
                if is_image(j, IMAGES - 1):
                    sum_up(j)
                for n in range(27):
                    m = n - 1
                    if 0 <= m < 24:
                        w = width(m // 12)
                        r = TAIL_W if m % 3 == 2 else MAIN
                        g = m // 3
                        dve.wait_ge(S["silu_done"], 24 * j + m + 1)
                        dve.wait_ge(S["h3_ps"], 24 * j + m + 1)
                        if g >= 2:
                            dve.wait_ge(S["y_ps"], 8 * j + g - 1)
                        V.tensor_tensor(hh[0:r, g % 2, m % 3, 0:w], su[0:r, m % 2, 0:w],
                                        P[0:r, 4 + m % 2, 0:w], ALU.mult).then_inc(S["hh_ready"], 1)
                    if n % 3 == 2 and n > 2:
                        g = n // 3 - 1
                        w = width(g // 4)
                        dve.wait_ge(S["y_ps"], 8 * j + g + 1)
                        dve.wait_ge(S["bw_saved"], 8 * j + g + 1)
                        if g >= 2:
                            dve.wait_ge(S["z_added"], 8 * j + g - 1)
                        V.tensor_tensor(zz[:, g % 2, 0:w], bw[:, g % 2, 0:w], P[:, 6, 0:w],
                                        ALU.mult).then_inc(S["z_ready"], 1)
                    yield

            def finish(j):
                dve.wait_ge(S["fold_ps"], j + 1)
                dve.wait_ge(S["out_sent"], j * 16 + 16)
                V.tensor_tensor(res[:], rest[:], tiles(6), ALU.add).then_inc(S["out_ready"], 1)
                dve.wait_ge(S["out_ready"], j + 2)
                yield

            second_pass(dve, memory, prepare, maxima, scores, after, route, experts, finish)


PIECES = [(kb, q0, q1) for kb in range(NT)
          for q0, q1 in (((kb * TP, 448), (448, TOK)) if kb < 4 else ((kb * TP, TOK),))]


def first_piece(kb):
    return next(n for n, p in enumerate(PIECES) if p[0] == kb)


def lay_out(x, L0_tok_W, L0_tok_b, L0_attn_Wk, L0_attn_Wq, L0_attn_Wv, L0_attn_Wlr, L0_attn_blr, L0_attn_Ws,
            L0_attn_bs, L0_ffn_ln1_w, L0_ffn_ln2_w, L0_ffn_wq, L0_ffn_wk, L0_ffn_wv, L0_ffn_wo, L0_ffn_router_w,
            L0_ffn_w1, L0_ffn_w2, L0_ffn_w3):
    n = SIDE
    patches = x.reshape(IMAGES, n, PATCH, n, PATCH).transpose(2, 4, 0, 1, 3).reshape(D, IMAGES * TOK)
    col = lambda a: a.reshape(1, -1)
    zero = lambda *s: np.zeros(s, np.float32)
    wproj = np.concatenate([
        np.concatenate([L0_attn_Wk, L0_attn_Wv, L0_attn_Wlr], 1),
        np.concatenate([zero(1, 2 * D), col(L0_attn_blr)], 1)], 0)
    half = HD // 2
    swap = (np.arange(QK) // HD) * HD + (np.arange(QK) % HD + half) % HD
    wqk = np.concatenate([L0_ffn_wq, L0_ffn_wk], 0)
    attnw = np.concatenate([wqk, wqk[swap], L0_ffn_wv], 0).T
    pairs = []
    for w in (L0_ffn_w1, L0_ffn_w3):
        for p in range(PAIRS):
            e, f = w[2 * p], w[2 * p + 1]
            pairs += [e[:MAIN], f[:MAIN], e[MAIN:], zero(64 - TAIL, D), f[MAIN:]]
    w13 = np.concatenate(pairs, 0).T
    w2 = zero(128, 3 * PAIRS, D)
    for p in range(PAIRS):
        for k in range(2):
            t = L0_ffn_w2[2 * p + k].T
            w2[:, 3 * p + k] = t[:MAIN]
            w2[64 * k:64 * k + TAIL, 3 * p + 2] = t[MAIN:]
    wo = zero(128, D)
    for h in range(NH):
        wo[32 * h:32 * h + HD] = L0_ffn_wo[:, h * HD:(h + 1) * HD].T
    con, rope = shape_constants()
    out = {
        "con": con, "rope": rope, "patches": patches,
        "tokw": np.concatenate([L0_tok_W.T, col(L0_tok_b)], 0),
        "wk_t": L0_attn_Wk.T, "wq_t": L0_attn_Wq.T, "w1l_t": L0_attn_Ws[1].T,
        "ws": np.concatenate([L0_attn_Ws.transpose(1, 0, 2), L0_attn_bs[None]], 0),
        "wproj": wproj, "wqp": np.concatenate([L0_attn_Wq, zero(1, D)], 0),
        "attnw": attnw, "router": L0_ffn_router_w.T, "lnw": np.stack([L0_ffn_ln1_w, L0_ffn_ln2_w], 1),
        "w13": w13, "w2": w2, "wo": wo,
    }
    return {k: np.ascontiguousarray(v) for k, v in out.items()}


def kernel(**inputs):
    import concourse.bacc as bacc
    from concourse.bass_utils import run_bass_kernel_spmd

    arrays = lay_out(**{k: np.asarray(v) for k, v in inputs.items()})
    nc = bacc.Bacc("TRN2", target_bir_lowering=False, num_devices=1)
    aps = {k: nc.dram_tensor(f"in_{k}", v.shape, F32, kind="ExternalInput").ap() for k, v in arrays.items()}
    out = nc.dram_tensor("out_tokens", (IMAGES * TOK, D), F32, kind="ExternalOutput").ap()
    aps["out"] = out.rearrange("(t p) f -> p t f", p=TP)
    vit_block(nc, aps)
    r = run_bass_kernel_spmd(nc, [{f"in_{k}": v for k, v in arrays.items()}], core_ids=[0])
    return r.results[0]["out_tokens"].reshape(IMAGES, TOK, D)
```
